# Optimizing a Trainium2 kernel written in Bass

```python
import numpy as np
import jax
import jax.numpy as jnp

def _softmax(x, axis=-1):
    return jax.nn.softmax(x, axis=axis)

def _gelu(x):
    return jax.nn.gelu(x, approximate=True)

def _silu(x):
    return jax.nn.silu(x)

def _sigmoid(x):
    return jax.nn.sigmoid(x)

def _layernorm(x, axis=-1, eps=1e-05):
    m = jnp.mean(x, axis=axis, keepdims=True)
    v = jnp.var(x, axis=axis, keepdims=True)
    return (x - m) / jnp.sqrt(v + eps)

def _scatter_add(tgt, idx, src, axis=0):
    return tgt.at[idx].add(src)

def _segment_sum(src, seg, n):
    return jax.ops.segment_sum(src, seg, n)
kernel_name = 'mk_prb_d1_jaxref_r8_7fc496'

def setup_inputs(seed: int=0):
    np.random.seed(seed)
    _w = jnp.asarray

    def _L0_attn_setup():
        import jax, jax.numpy as jnp
        import numpy as np
        NUM_HEADS = 16
        WINDOW = 128
        PERSIST = 16
        key = jax.random.key(seed)
        ks = jax.random.split(key, 6)
        B, S, D, L = (2, 256, 256, 64)
        sd = 1.0 / np.sqrt(D)
        sl = 1.0 / np.sqrt(L)
        return {'x': jax.random.normal(ks[0], (B, S, D), dtype=jnp.float32), 'Wq': jax.random.normal(ks[1], (D, D), dtype=jnp.float32) * sd, 'Wkv': jax.random.normal(ks[2], (D, L), dtype=jnp.float32) * sd, 'Wk': jax.random.normal(ks[3], (L, D), dtype=jnp.float32) * sl, 'Wv': jax.random.normal(ks[4], (L, D), dtype=jnp.float32) * sl, 'Wo': jax.random.normal(ks[5], (D, D), dtype=jnp.float32) * sd}
    _L0_attn_in = _L0_attn_setup()

    def _L0_ffn_setup():
        import jax, jax.numpy as jnp
        import numpy as np
        BLOCK_SIZE = 32
        HIDDEN_SIZE = 256
        MLP_DIM = 2048
        NVFP4_LUT = jnp.array([0.0, 0.5, 1.0, 1.5, 2.0, 3.0, 4.0, 6.0, 0.0, -0.5, -1.0, -1.5, -2.0, -3.0, -4.0, -6.0], dtype=jnp.float32)

        def dequant_nvfp4(W_packed, scales, block=BLOCK_SIZE):
            N = W_packed.shape[0]
            low = W_packed & 15
            high = W_packed >> 4 & 15
            idx = jnp.stack([low, high], axis=-1).reshape(N, -1)
            vals = NVFP4_LUT[idx]
            K = vals.shape[1]
            vals = vals.reshape(N, K // block, block) * scales[:, :, None]
            return vals.reshape(N, K)
        key = jax.random.key(seed)
        ks = jax.random.split(key, 7)
        x = jax.random.normal(ks[0], (4, 32, HIDDEN_SIZE), dtype=jnp.float32)
        gate_W_packed = jax.random.randint(ks[1], (MLP_DIM, HIDDEN_SIZE // 2), 0, 32, dtype=jnp.int32)
        gate_scales = jax.random.uniform(ks[2], (MLP_DIM, HIDDEN_SIZE // BLOCK_SIZE), dtype=jnp.float32) * 0.1 + 0.001
        up_W_packed = jax.random.randint(ks[3], (MLP_DIM, HIDDEN_SIZE // 2), 0, 32, dtype=jnp.int32)
        up_scales = jax.random.uniform(ks[4], (MLP_DIM, HIDDEN_SIZE // BLOCK_SIZE), dtype=jnp.float32) * 0.1 + 0.001
        down_W_packed = jax.random.randint(ks[5], (HIDDEN_SIZE, MLP_DIM // 2), 0, 32, dtype=jnp.int32)
        down_scales = jax.random.uniform(ks[6], (HIDDEN_SIZE, MLP_DIM // BLOCK_SIZE), dtype=jnp.float32) * 0.1 + 0.001
        return {'x': x, 'gate_W_packed': gate_W_packed, 'gate_scales': gate_scales, 'up_W_packed': up_W_packed, 'up_scales': up_scales, 'down_W_packed': down_W_packed, 'down_scales': down_scales}
    _L0_ffn_in = _L0_ffn_setup()
    _d = {'L0_attn_x': _L0_attn_in['x'], 'L0_attn_Wq': _L0_attn_in['Wq'], 'L0_attn_Wkv': _L0_attn_in['Wkv'], 'L0_attn_Wk': _L0_attn_in['Wk'], 'L0_attn_Wv': _L0_attn_in['Wv'], 'L0_attn_Wo': _L0_attn_in['Wo'], 'L0_ffn_gate_W_packed': _L0_ffn_in['gate_W_packed'], 'L0_ffn_gate_scales': _L0_ffn_in['gate_scales'], 'L0_ffn_up_W_packed': _L0_ffn_in['up_W_packed'], 'L0_ffn_up_scales': _L0_ffn_in['up_scales'], 'L0_ffn_down_W_packed': _L0_ffn_in['down_W_packed'], 'L0_ffn_down_scales': _L0_ffn_in['down_scales']}
    _x0 = _d['L0_attn_x']
    _d['L0_attn_x'] = jax.random.normal(jax.random.fold_in(jax.random.key(seed), 1), (16, 256, 256), dtype=_x0.dtype)
    del _x0
    return _d

def reference(L0_attn_x, L0_attn_Wq, L0_attn_Wkv, L0_attn_Wk, L0_attn_Wv, L0_attn_Wo, L0_ffn_gate_W_packed, L0_ffn_gate_scales, L0_ffn_up_W_packed, L0_ffn_up_scales, L0_ffn_down_W_packed, L0_ffn_down_scales):

    def _L0_attn_ref(x, Wq, Wkv, Wk, Wv, Wo):
        import jax, jax.numpy as jnp
        import numpy as np
        NUM_HEADS = 16
        WINDOW = 128
        PERSIST = 16
        B, S, D = x.shape
        H = NUM_HEADS
        hd = D // H
        scale = hd ** (-0.5)
        q = (x @ Wq).reshape(B, S, H, hd)
        kv_latent = x @ Wkv
        k = (kv_latent @ Wk).reshape(B, S, H, hd)
        v = (kv_latent @ Wv).reshape(B, S, H, hd)
        qi = jnp.arange(S)[:, None]
        ki = jnp.arange(S)[None, :]
        mask = (ki <= qi) & ((qi - ki < WINDOW) | (ki < PERSIST))
        scores = jnp.einsum('bqhd,bkhd->bhqk', q, k) * scale
        scores = jnp.where(mask[None, None], scores, jnp.finfo(scores.dtype).min)
        attn = jax.nn.softmax(scores, axis=-1)
        out = jnp.einsum('bhqk,bkhd->bqhd', attn, v).reshape(B, S, D)
        return out @ Wo

    def _L0_ffn_ref(x, gate_W_packed, gate_scales, up_W_packed, up_scales, down_W_packed, down_scales):
        import jax, jax.numpy as jnp
        import numpy as np
        BLOCK_SIZE = 32
        HIDDEN_SIZE = 256
        MLP_DIM = 2048
        NVFP4_LUT = jnp.array([0.0, 0.5, 1.0, 1.5, 2.0, 3.0, 4.0, 6.0, 0.0, -0.5, -1.0, -1.5, -2.0, -3.0, -4.0, -6.0], dtype=jnp.float32)

        def dequant_nvfp4(W_packed, scales, block=BLOCK_SIZE):
            N = W_packed.shape[0]
            low = W_packed & 15
            high = W_packed >> 4 & 15
            idx = jnp.stack([low, high], axis=-1).reshape(N, -1)
            vals = NVFP4_LUT[idx]
            K = vals.shape[1]
            vals = vals.reshape(N, K // block, block) * scales[:, :, None]
            return vals.reshape(N, K)
        B, S, H = x.shape
        xt = x.reshape(B * S, H)
        Wg = dequant_nvfp4(gate_W_packed, gate_scales)
        Wu = dequant_nvfp4(up_W_packed, up_scales)
        Wd = dequant_nvfp4(down_W_packed, down_scales)
        gate = jnp.einsum('th,nh->tn', xt, Wg)
        up = jnp.einsum('th,nh->tn', xt, Wu)
        gelu = jnp.tanh(0.7978845608028654 * (gate + 0.044715 * gate ** 3)) * gate * 0.5 + gate * 0.5
        inter = gelu * up
        out = jnp.einsum('tn,hn->th', inter, Wd)
        return out.reshape(B, S, H)
    x = L0_attn_x
    xn = _layernorm(x, axis=-1)
    x = x + _L0_attn_ref(xn, L0_attn_Wq, L0_attn_Wkv, L0_attn_Wk, L0_attn_Wv, L0_attn_Wo) + _L0_ffn_ref(xn, L0_ffn_gate_W_packed, L0_ffn_gate_scales, L0_ffn_up_W_packed, L0_ffn_up_scales, L0_ffn_down_W_packed, L0_ffn_down_scales)
    return x

_drawn_inputs = setup_inputs


def setup_inputs(seed=0):
    import zlib

    import numpy as np

    out = dict(_drawn_inputs(seed))
    spreads = {}
    factors = {'L0_attn_Wq': 4.136,
     'L0_attn_Wkv': 3.655,
     'L0_attn_Wk': 4.073,
     'L0_attn_Wv': 3.184,
     'L0_attn_Wo': 3.235}
    for name, (base, spread) in spreads.items():
        noise = np.random.default_rng([zlib.crc32(name.encode()), seed]).standard_normal(out[name].shape)
        drawn = base * np.exp(spread * noise) if base else spread * noise
        out[name] = jnp.asarray(drawn.astype(out[name].dtype))
    for name, factor in factors.items():
        out[name] = (out[name] * factor).astype(out[name].dtype)
    return out
```

```python
import numpy as np

import concourse.bass as bass
import concourse.mybir as mybir
from concourse.alu_op_type import AluOpType as ALU
from contextlib import ExitStack

ACT = mybir.ActivationFunctionType
F32, F16, U16, I32 = mybir.dt.float32, mybir.dt.float16, mybir.dt.uint16, mybir.dt.int32

P = 128
B, S, D = 16, 256, 256
H, HD = 16, 16
L = 64
WINDOW, PERSIST = 128, 16
MLP, BLOCK = 2048, 32
TT = S // P
KT = D // P
STEPS = 16
CHUNKS = MLP // (2 * P)
IN_FLIGHT = 4
GROUPS = 4
EPS = 1e-5
UP = 256.0
DOWN = 1.0 / UP
MASKED = -1e30
GELU_CUBE = 0.044715
GELU_SLOPE = 0.7978845608028654
GATE, UPW, DOWNW = range(3)


def head_of(step):
    group, quadrant = divmod(step, 4)
    return 8 * (group // 2) + 2 * quadrant + group % 2


def some(count):
    return not isinstance(count, int) or count > 0


def layer(nc, x, wq, wkv, wk, wv, wo, packed, scales, out):
    ctx = ExitStack()
    with ctx:
        def sb(name, shape, dtype=F32):
            return ctx.enter_context(nc.sbuf_tensor(name, shape, dtype))

        def bank(name):
            return ctx.enter_context(nc.psum_tensor(name, [P, 512], F32))

        def sem(name):
            return ctx.enter_context(nc.semaphore(name))

        ident = sb("ident", [P, P])
        mask = sb("mask", [P, 3 * P])
        x_in = sb("x_in", [P, TT, D])
        x_res = sb("x_res", [P, TT, D])
        bn = sb("bn", [P, TT, 6])
        mv = sb("mv", [P, TT, 2])
        nm = sb("nm", [P, TT])
        ve = sb("ve", [P, TT])
        minus_half = sb("minus_half", [P, TT])
        rstd = sb("rstd", [P, TT])
        xn = sb("xn", [P, TT, D])
        xT_hi = sb("xT_hi", [P, 2, KT, S], F16)
        xT_lo = sb("xT_lo", [P, 2, KT, S], F16)
        A_WQ, A_WKV, A_WK, A_WV, A_WO, A_END = 0, 512, 768, 1024, 1280, 1792
        aw = sb("aw", [P, A_END])
        aw_hi = sb("aw_hi", [P, A_END], F16)
        aw_lo = sb("aw_lo", [P, A_END], F16)
        lat = sb("lat", [P, S], F16)
        q_hi = sb("q_hi", [P, 2, S], F16)
        q_lo = sb("q_lo", [P, 2, S], F16)
        k_hi = sb("k_hi", [P, 2, S], F16)
        k_lo = sb("k_lo", [P, 2, S], F16)
        q_stack = sb("q_stack", [P, 2, H // 2, S], F16)
        k_stack = sb("k_stack", [P, 2, H // 2, S], F16)
        v_pad = sb("v_pad", [P, 2, TT, H, 2 * HD])
        s_neg = sb("s_neg", [P, 2, 3 * P])
        nmax = sb("nmax", [P, 2, TT])
        probs = sb("probs", [P, 2, 3 * P])
        rowsum = sb("rowsum", [P, 2, TT])
        rrow = sb("rrow", [P, 2, TT])
        pT = sb("pT", [P, 8, 3 * P])
        o_hi = sb("o_hi", [P, 2, S], F16)
        o_lo = sb("o_lo", [P, 2, S], F16)
        sq = sb("sq", [P, 2, S])
        poly = sb("poly", [P, 2, S])
        th = sb("th", [P, 2, S])
        gelu = sb("gelu", [P, 2, S])
        inter = sb("inter", [P, 2, S])
        i_hi = sb("i_hi", [P, 4, S], F16)
        i_lo = sb("i_lo", [P, 4, S], F16)
        ffn = sb("ffn", [P, TT * D])
        o_sb = sb("o_sb", [P, TT * D])
        pk = sb("pk", [P, IN_FLIGHT, 3 * S], I32)
        sc = sb("sc", [P, IN_FLIGHT, 3 * S])
        code = sb("code", [P, 2, 3 * S], U16)
        sign = sb("sign", [P, 2, 3 * S], U16)
        low = sb("low", [P, 2, 3 * S], F16)
        wf = sb("wf", [P, 2, 2, 3 * S])
        w_hi = sb("w_hi", [P, CHUNKS, 2, 3, S], F16)
        w_lo = sb("w_lo", [P, CHUNKS, 2, 3, S], F16)
        q_dram = nc.dram_tensor("q_rows", [2, H, 2, HD, S], F16, kind="Internal").ap()
        k_dram = nc.dram_tensor("k_rows", [2, H, 3, HD, S], F16, kind="Internal").ap()

        gu = [bank("gu0"), bank("gu1")]
        acc = bank("acc")
        sc_ps = bank("sc_ps")
        pT_ps = bank("pT_ps")
        o_ps = bank("o_ps")
        m0 = bank("m0")
        m1 = bank("m1")

        aw_loaded, aw_hi_done, aw_ready = sem("aw_loaded"), sem("aw_hi_done"), sem("aw_ready")
        pk_loaded = [sem(f"pk_loaded{c}") for c in range(CHUNKS)]
        decode = sem("decode")
        w_float, w_hi_done, w_ready = sem("w_float"), sem("w_hi_done"), sem("w_ready")
        const_step, const_ready = sem("const_step"), sem("const_ready")
        passed = sem("passed")
        x_loaded, res_loaded = sem("x_loaded"), sem("res_loaded")
        bn_done, aggr_done, stats_ready = sem("bn_done"), sem("aggr_done"), sem("stats_ready")
        rstd_done, xn_ready = sem("rstd_done"), sem("xn_ready")
        x_transposed, x_hi_done, x_split = sem("x_transposed"), sem("x_hi_done"), sem("x_split")
        lat_done, lat_hi_done, lat_split = sem("lat_done"), sem("lat_hi_done"), sem("lat_split")
        q_done, q_hi_done, q_split = sem("q_done"), sem("q_hi_done"), sem("q_split")
        k_done, k_hi_done, k_split = sem("k_done"), sem("k_hi_done"), sem("k_split")
        v_done, v_stored = sem("v_done"), sem("v_stored")
        q_rows_stored, k_rows_stored = sem("q_rows_stored"), sem("k_rows_stored")
        stack_loaded = sem("stack_loaded")
        scores_done, max_done, exp_done = sem("scores_done"), sem("max_done"), sem("exp_done")
        recip_done, normed = sem("recip_done"), sem("normed")
        pT_done, pT_stored, pv_done = sem("pT_done"), sem("pT_stored"), sem("pv_done")
        o_hi_done, o_split, wo_done = sem("o_hi_done"), sem("o_split"), sem("wo_done")
        gu_done, sq_done, poly_done = sem("gu_done"), sem("sq_done"), sem("poly_done")
        th_done, gelu_done, inter_done = sem("th_done"), sem("gelu_done"), sem("inter_done")
        i_hi_done, i_split, down_done = sem("i_hi_done"), sem("i_split"), sem("down_done")
        ffn_done, out_ready, out_stored = sem("ffn_done"), sem("out_ready"), sem("out_stored")

        def alone(eng):
            eng.sem_inc(passed, 1)

        x_tok = x.rearrange("b (t p) d -> b p t d", p=P)
        out_tok = out.rearrange("b (t p) d -> b p t d", p=P)
        Q_LOADS, STACK_LOADS = 2 * 2, 2 * 2 * 2
        Q_STORES, K_STORES = 2 * 2, 3 * 2

        block = ctx.enter_context(nc.Block())

        @block.sync
        def _(sp):
            def load_tokens(b):
                sp.dma_start(x_in[:, :, :], x_tok[b]).then_inc(x_loaded, 16)

            def store_rows(b, par):
                sp.wait_ge(q_split, b + 1)
                for piece, src in enumerate((q_hi, q_lo)):
                    for t in range(2):
                        sp.dma_start(q_dram[par, 8 * t:8 * t + 8, piece],
                                     src[:, t, :]).then_inc(q_rows_stored, 16)
                sp.wait_ge(k_split, b + 1)
                for piece, src in enumerate((k_hi, k_lo, k_hi)):
                    for t in range(2):
                        sp.dma_start(k_dram[par, 8 * t:8 * t + 8, piece],
                                     src[:, t, :]).then_inc(k_rows_stored, 16)

            def load_stacks(b, par):
                sp.wait_ge(q_rows_stored, 16 * Q_STORES * (b + 1))
                for dst, src, offset in ((q_stack, q_dram, 0), (k_stack, k_dram, 1)):
                    if offset:
                        sp.wait_ge(k_rows_stored, 16 * K_STORES * (b + 1))
                    for half in range(2):
                        for odd in range(2):
                            rows = src[par, odd:H:2, half * offset:half * offset + 2]
                            sp.dma_start(dst[64 * odd + 32 * half:64 * odd + 32 * half + 32, par, :, :],
                                         rows.rearrange("h c d t -> (c d) h t")).then_inc(stack_loaded, 16)

            def batch(b, par, first, last):
                if not (first or last):
                    sp.wait_ge(xn_ready, b + 1)
                    alone(sp)
                    load_tokens(b + 1)
                if some(b):
                    sp.wait_ge(ffn_done, b)
                alone(sp)
                sp.dma_start(x_res[:, :, :], x_tok[b]).then_inc(res_loaded, 16)
                if not first:
                    if some(b):
                        sp.wait_ge(out_ready, b)
                    alone(sp)
                    sp.dma_start(out_tok[b - 1], o_sb[:, :].rearrange("p (t d) -> p t d", t=TT)).then_inc(out_stored, 16)
                if not last:
                    store_rows(b + 1, 1 - par)
                    if some(STEPS * b):
                        sp.wait_ge(scores_done, STEPS * b)
                    alone(sp)
                    load_stacks(b + 1, 1 - par)

            load_tokens(0)
            for dst, src in ((aw[:, A_WQ:A_WKV].rearrange("p (t n) -> p t n", t=KT), wq.rearrange("(p t) n -> p t n", t=KT)),
                             (aw[0:L, A_WK:A_WV], wk), (aw[L:P, A_WK:A_WV], wk),
                             (aw[0:L, A_WV:A_WO], wv), (aw[L:P, A_WV:A_WO], wv),
                             (aw[:, A_WO:A_END].rearrange("p (t n) -> p t n", t=2), wo.rearrange("(t p) n -> p t n", t=2))):
                sp.dma_start(dst, src).then_inc(aw_loaded, 16)
            kv4 = aw[:, A_WKV:A_WK].rearrange("p (t c n) -> p t c n", t=KT, c=2)
            for c in range(2):
                sp.dma_start(kv4[:, :, c, :], wkv.rearrange("(p t) n -> p t n", t=KT)).then_inc(aw_loaded, 16)

            def load_chunk(c):
                if some(c - IN_FLIGHT + 1):
                    sp.wait_ge(w_float, c - IN_FLIGHT + 1)
                sp.dma_start(pk[:, c % IN_FLIGHT, :], packed[:, c, :]).then_inc(pk_loaded[c], 16)
                for g in range(P // 16):
                    sp.dma_start(sc[16 * g:16 * g + 16, c % IN_FLIGHT, :],
                                 scales[g:g + 1, c, :].to_broadcast([16, 3 * S])).then_inc(pk_loaded[c], 16)

            for c in range(IN_FLIGHT):
                load_chunk(c)
            sp.wait_ge(xn_ready, 1)
            load_tokens(1)
            store_rows(0, 0)
            load_stacks(0, 0)
            for c in range(IN_FLIGHT, CHUNKS):
                load_chunk(c)
            batch(0, 0, True, False)
            with sp.Fori(0, (B - 2) // 2) as it:
                batch(2 * it + 1, 1, False, False)
                batch(2 * it + 2, 0, False, False)
            batch(B - 1, 1, False, True)
            sp.wait_ge(out_ready, B)
            sp.dma_start(out_tok[B - 1], o_sb[:, :].rearrange("p (t d) -> p t d", t=TT)).then_inc(out_stored, 16)
            sp.wait_ge(out_stored, 16 * B)

        @block.gpsimd
        def _(pool):
            def weights_lo(c):
                pool.wait_ge(w_hi_done, c + 1)
                nc.gpsimd.tensor_tensor(w_lo[:, c].rearrange("p a m n -> p (a m n)"),
                                        wf[:, c % 2].rearrange("p a n -> p (a n)"),
                                        w_hi[:, c].rearrange("p a m n -> p (a m n)"), ALU.subtract).then_inc(w_ready, 1)

            def norm_tokens(b):
                pool.wait_ge(stats_ready, 2 * (b + 1))
                nc.gpsimd.tensor_tensor(rstd[:, :], ve[:, :], minus_half[:, :], ALU.pow).then_inc(rstd_done, 1)
                pool.wait_ge(rstd_done, b + 1)
                if some(b):
                    pool.wait_ge(x_transposed, b)
                alone(pool)
                for t in range(TT):
                    op = nc.gpsimd.tensor_scalar(xn[:, t, :], x_in[:, t, :], nm[:, t:t + 1], rstd[:, t:t + 1],
                                                 ALU.add, ALU.mult)
                op.then_inc(xn_ready, 1)

            def intermediate_lo(n, i):
                pool.wait_ge(i_hi_done, n + 1)
                nc.gpsimd.tensor_tensor(i_lo[:, i % 4, :], inter[:, i % 2, :], i_hi[:, i % 4, :],
                                        ALU.subtract).then_inc(i_split, 1)

            def scale_probs(n, i):
                pool.wait_ge(recip_done, n + 1)
                alone(pool)
                r = i % 2
                nc.gpsimd.tensor_scalar(probs[:, r, 0:P], probs[:, r, 0:P], rrow[:, r, 0:1], 1.0, ALU.mult, ALU.mult)
                nc.gpsimd.tensor_scalar(probs[:, r, P:3 * P], probs[:, r, P:3 * P], rrow[:, r, 1:2], 1.0,
                                        ALU.mult, ALU.mult).then_inc(normed, 1)

            def batch(b, par, first, last):
                for i in range(STEPS):
                    n = STEPS * b + i
                    if not (first and i == 0):
                        intermediate_lo(n - 1, (i - 1) % STEPS)
                    scale_probs(n, i)
                    if i == 1 and not last:
                        norm_tokens(b + 1)
                    if first and i % 2 == 1 and (i + 3) // 2 < CHUNKS:
                        weights_lo((i + 3) // 2)

            nc.gpsimd.memset(ident[:, :], 0.0).then_inc(const_step, 1)
            nc.gpsimd.memset(mask[:, :], 0.0).then_inc(const_step, 1)
            nc.gpsimd.memset(minus_half[:, :], -0.5).then_inc(const_step, 1)
            nc.gpsimd.memset(v_pad[:, :, :, :, :], 0.0).then_inc(const_ready, 1)
            pool.wait_ge(const_step, 3)
            nc.gpsimd.affine_select(out=ident[:, :], in_=ident[:, :], compare_op=ALU.not_equal, fill=1.0, base=0,
                                    pattern=[[-1, P]], channel_multiplier=1).then_inc(const_ready, 1)
            for c0 in (0, 2 * P):
                nc.gpsimd.affine_select(out=mask[:, c0:c0 + P], in_=mask[:, c0:c0 + P], compare_op=ALU.is_ge,
                                        fill=MASKED, base=0, pattern=[[-1, P]], channel_multiplier=1).then_inc(const_ready, 1)
            nc.gpsimd.affine_select(out=mask[:, P + PERSIST:2 * P], in_=mask[:, P + PERSIST:2 * P], compare_op=ALU.is_ge,
                                    fill=MASKED, base=PERSIST - (P - WINDOW) - 1, pattern=[[1, P - PERSIST]],
                                    channel_multiplier=-1).then_inc(const_ready, 1)
            norm_tokens(0)
            weights_lo(0)
            weights_lo(1)
            batch(0, 0, True, False)
            with pool.Fori(0, (B - 2) // 2) as it:
                batch(2 * it + 1, 1, False, False)
                batch(2 * it + 2, 0, False, False)
            batch(B - 1, 1, False, True)
            intermediate_lo(STEPS * B - 1, STEPS - 1)

        @block.scalar
        def _(act):
            def hi_piece(dst, src, scale, done):
                nc.scalar.activation(dst, src, ACT.Copy, scale=scale).then_inc(done, 1)

            def weights_hi(c):
                act.wait_ge(w_float, c + 1)
                hi_piece(w_hi[:, c].rearrange("p a m n -> p (a m n)"), wf[:, c % 2].rearrange("p a n -> p (a n)"), 1.0, w_hi_done)

            def tokens_hi(b, par):
                act.wait_ge(x_transposed, b + 1)
                hi_piece(xT_hi[:, par], m0[:, :].rearrange("p (t s) -> p t s", t=KT), 1.0, x_hi_done)

            def latent_hi(b):
                if some(b):
                    act.wait_ge(v_done, b)
                act.wait_ge(lat_done, b + 1)
                hi_piece(lat[:, :], m0[:, 0:S], DOWN, lat_hi_done)

            def queries_hi(b):
                if some(16 * Q_STORES * b):
                    act.wait_ge(q_rows_stored, 16 * Q_STORES * b)
                act.wait_ge(q_done, b + 1)
                hi_piece(q_hi[:, :, :], m1[:, :].rearrange("p (t s) -> p t s", t=2), DOWN, q_hi_done)

            def keys_hi(b):
                if some(16 * K_STORES * b):
                    act.wait_ge(k_rows_stored, 16 * K_STORES * b)
                act.wait_ge(k_done, b + 1)
                hi_piece(k_hi[:, :, :], m0[:, :].rearrange("p (t s) -> p t s", t=2), DOWN, k_hi_done)

            def values_store(b, par, t):
                act.wait_ge(v_done, b + 1)
                if some(GROUPS * (b - 1)):
                    act.wait_ge(pv_done, GROUPS * (b - 1))
                for odd in range(2):
                    dst = v_pad[:, par, t, odd:H:2, HD * odd:HD * odd + HD]
                    src = m1[:, D * t:D * t + D].rearrange("p (h d) -> p h d", d=HD)[:, odd:H:2, :]
                    hi_piece(dst, src, DOWN, v_stored)

            def attention_hi(b):
                if some(b):
                    act.wait_ge(wo_done, b)
                act.wait_ge(pv_done, GROUPS * (b + 1))
                hi_piece(o_hi[:, :, :], o_ps[:, :].rearrange("p (t s) -> p t s", t=2), 1.0, o_hi_done)

            def exponentials(n, i):
                if some(n - 1):
                    act.wait_ge(pT_done, n - 1)
                act.wait_ge(max_done, 2 * (n + 1))
                r = i % 2
                nc.scalar.activation(probs[:, r, 0:P], s_neg[:, r, 0:P], ACT.Exp, bias=nmax[:, r, 0:1], scale=-1.0,
                                     accum_out=rowsum[:, r, 0:1])
                nc.scalar.activation(probs[:, r, P:3 * P], s_neg[:, r, P:3 * P], ACT.Exp, bias=nmax[:, r, 1:2], scale=-1.0,
                                     accum_out=rowsum[:, r, 1:2]).then_inc(exp_done, 1)

            def squares(n, i):
                act.wait_ge(gu_done, n + 1)
                nc.scalar.activation(sq[:, i % 2, :], gu[i % 2][:, 0:S], ACT.Square,
                                     scale=GELU_CUBE ** 0.5 * DOWN).then_inc(sq_done, 1)

            def tanhs(n, i):
                act.wait_ge(poly_done, n + 1)
                nc.scalar.activation(th[:, i % 2, :], poly[:, i % 2, :], ACT.Tanh, scale=GELU_SLOPE * DOWN).then_inc(th_done, 1)

            def store_pT(b, i):
                n = STEPS * b + i
                if i % 4 == 0:
                    if some(GROUPS * b + i // 4 - 1):
                        act.wait_ge(pv_done, GROUPS * b + i // 4 - 1)
                act.wait_ge(pT_done, n + 1)
                nc.scalar.activation(pT[:, i % 8, :], pT_ps[:, 0:3 * P], ACT.Copy).then_inc(pT_stored, 1)

            def batch(b, par, first, last):
                for i in range(STEPS):
                    n = STEPS * b + i
                    exponentials(n, i)
                    squares(n, i)
                    if not (first and i == 0):
                        if i == 0:
                            store_pT(b - 1, STEPS - 1)
                        else:
                            store_pT(b, i - 1)
                    if i == 2 and not first:
                        attention_hi(b - 1)
                    if not last:
                        if i == 3:
                            tokens_hi(b + 1, 1 - par)
                        if i == 6:
                            latent_hi(b + 1)
                        if i == 8:
                            queries_hi(b + 1)
                        if i == 10:
                            keys_hi(b + 1)
                        if i in (11, 12):
                            values_store(b + 1, 1 - par, i - 11)
                    tanhs(n, i)
                    if first and i % 2 == 1 and (i + 3) // 2 < CHUNKS:
                        weights_hi((i + 3) // 2)

            act.wait_ge(aw_loaded, 16 * 8)
            hi_piece(aw_hi[:, :], aw[:, :], UP, aw_hi_done)
            act.wait_ge(const_ready, 5)
            tokens_hi(0, 0)
            latent_hi(0)
            queries_hi(0)
            weights_hi(0)
            keys_hi(0)
            values_store(0, 0, 0)
            values_store(0, 0, 1)
            weights_hi(1)
            batch(0, 0, True, False)
            with act.Fori(0, (B - 2) // 2) as it:
                batch(2 * it + 1, 1, False, False)
                batch(2 * it + 2, 0, False, False)
            batch(B - 1, 1, False, True)
            store_pT(B - 1, STEPS - 1)
            attention_hi(B - 1)

        @block.vector
        def _(dve):
            decoded = [0]

            def link(op):
                decoded[0] += 1
                op.then_inc(decode, 1)
                dve.wait_ge(decode, decoded[0])

            def decode_chunk(c):
                dve.wait_ge(pk_loaded[c], 16 * 9)
                byte = pk[:, c % IN_FLIGHT, :].bitcast(U16).rearrange("p (n two) -> p n two", two=2)[:, :, 0]
                for nibble, shift in ((0, 9), (1, 5)):
                    nc.vector.tensor_scalar(code[:, nibble, :], byte, shift, 0x0E00, ALU.logical_shift_left, ALU.bitwise_and)
                for nibble, shift in ((0, 12), (1, 8)):
                    op = nc.vector.tensor_scalar(sign[:, nibble, :], byte, shift, 0x8000, ALU.logical_shift_left, ALU.bitwise_and)
                link(op)
                code_all = code[:, :, :].rearrange("p a n -> p (a n)")
                sign_all = sign[:, :, :].rearrange("p a n -> p (a n)")
                low_all = low[:, :, :].rearrange("p a n -> p (a n)")
                link(nc.vector.tensor_scalar(code_all, code_all, 0x4000, None, ALU.bitwise_or))
                link(nc.vector.tensor_scalar(low_all, code_all.bitcast(F16), -4.0, 0.0, ALU.add, ALU.min))
                link(nc.vector.tensor_tensor(low_all, low_all, code_all.bitcast(F16), ALU.add))
                link(nc.vector.tensor_tensor(sign_all, sign_all, low_all.bitcast(U16), ALU.bitwise_xor))
                if some(c - 1):
                    dve.wait_ge(w_ready, c - 1)
                nc.vector.scalar_tensor_tensor(out=wf[:, c % 2], in0=sign[:, :, :].bitcast(F16), scalar=UP / 4.0,
                                               in1=sc[:, c % IN_FLIGHT:c % IN_FLIGHT + 1, :].to_broadcast([P, 2, 3 * S]),
                                               op0=ALU.mult, op1=ALU.mult).then_inc(w_float, 1)

            def lo_piece(dst, src, hi, scale, done):
                nc.vector.scalar_tensor_tensor(out=dst, in0=src, scalar=scale, in1=hi,
                                               op0=ALU.mult, op1=ALU.subtract).then_inc(done, 1)

            def stats(b):
                dve.wait_ge(x_loaded, 16 * (b + 1))
                for t in range(TT):
                    op = nc.vector.bn_stats(bn[:, t, :], x_in[:, t, :])
                op.then_inc(bn_done, 1)

            def moments(b):
                dve.wait_ge(bn_done, b + 1)
                alone(dve)
                for t in range(TT):
                    op = nc.vector.bn_aggr(mv[:, t, :], bn[:, t, :])
                op.then_inc(aggr_done, 1)
                dve.wait_ge(aggr_done, b + 1)
                nc.vector.tensor_scalar(nm[:, :], mv[:, :, 0], -1.0, None, ALU.mult).then_inc(stats_ready, 1)
                nc.vector.tensor_scalar(ve[:, :], mv[:, :, 1], EPS, None, ALU.add).then_inc(stats_ready, 1)

            def tokens_lo(b, par):
                dve.wait_ge(x_hi_done, b + 1)
                lo_piece(xT_lo[:, par], m0[:, :].rearrange("p (t s) -> p t s", t=KT), xT_hi[:, par], 1.0, x_split)

            def latent_lo(b):
                dve.wait_ge(lat_hi_done, b + 1)
                lo_piece(lat[L:P, :], m0[L:P, 0:S], lat[L:P, :], DOWN, lat_split)

            def queries_lo(b):
                dve.wait_ge(q_hi_done, b + 1)
                lo_piece(q_lo[:, :, :], m1[:, :].rearrange("p (t s) -> p t s", t=2), q_hi[:, :, :], DOWN, q_split)

            def keys_lo(b):
                dve.wait_ge(k_hi_done, b + 1)
                lo_piece(k_lo[:, :, :], m0[:, :].rearrange("p (t s) -> p t s", t=2), k_hi[:, :, :], DOWN, k_split)

            def attention_lo(b):
                dve.wait_ge(o_hi_done, b + 1)
                lo_piece(o_lo[:, :, :], o_ps[:, :].rearrange("p (t s) -> p t s", t=2), o_hi[:, :, :], 1.0, o_split)

            def add_ffn(b):
                dve.wait_ge(down_done, STEPS * (b + 1))
                dve.wait_ge(res_loaded, 16 * (b + 1))
                nc.vector.scalar_tensor_tensor(out=ffn[:, :], in0=acc[:, :], scalar=DOWN,
                                               in1=x_res[:, :, :].rearrange("p t d -> p (t d)"),
                                               op0=ALU.mult, op1=ALU.add).then_inc(ffn_done, 1)

            def add_attention(b):
                if some(16 * b):
                    dve.wait_ge(out_stored, 16 * b)
                dve.wait_ge(wo_done, b + 1)
                dve.wait_ge(ffn_done, b + 1)
                nc.vector.scalar_tensor_tensor(out=o_sb[:, :], in0=m1[:, :], scalar=DOWN, in1=ffn[:, :],
                                               op0=ALU.mult, op1=ALU.add).then_inc(out_ready, 1)

            def maxima(n, i):
                if some(n - 1):
                    dve.wait_ge(exp_done, n - 1)
                dve.wait_ge(scores_done, n + 1)
                alone(dve)
                r = i % 2
                for t, (c0, c1) in enumerate(((0, P), (P, 3 * P))):
                    nc.vector.tensor_tensor_reduce(out=s_neg[:, r, c0:c1], in0=sc_ps[:, c0:c1], in1=mask[:, c0:c1],
                                                   scale=-1.0 / HD ** 0.5, scalar=3e38, op0=ALU.add, op1=ALU.min,
                                                   accum_out=nmax[:, r, t:t + 1]).then_inc(max_done, 1)

            def reciprocals(n, i):
                dve.wait_ge(exp_done, n + 1)
                nc.vector.reciprocal(rrow[:, i % 2, :], rowsum[:, i % 2, :]).then_inc(recip_done, 1)

            def polynomial(n, i):
                dve.wait_ge(sq_done, n + 1)
                nc.vector.scalar_tensor_tensor(out=poly[:, i % 2, :], in0=sq[:, i % 2, :], scalar=1.0,
                                               in1=gu[i % 2][:, 0:S], op0=ALU.add, op1=ALU.mult).then_inc(poly_done, 1)

            def twice_gelu(n, i):
                dve.wait_ge(th_done, n + 1)
                nc.vector.scalar_tensor_tensor(out=gelu[:, i % 2, :], in0=th[:, i % 2, :], scalar=1.0,
                                               in1=gu[i % 2][:, 0:S], op0=ALU.add, op1=ALU.mult).then_inc(gelu_done, 1)

            def gated(n, i):
                if some(n - 1):
                    dve.wait_ge(i_split, n - 1)
                dve.wait_ge(gelu_done, n + 1)
                nc.vector.scalar_tensor_tensor(out=inter[:, i % 2, :], in0=gelu[:, i % 2, :], scalar=0.5 * DOWN * DOWN,
                                               in1=gu[i % 2][:, S:2 * S], op0=ALU.mult, op1=ALU.mult).then_inc(inter_done, 1)

            def intermediate_hi(n, i):
                if some(n - 3):
                    dve.wait_ge(down_done, n - 3)
                dve.wait_ge(inter_done, n + 1)
                nc.vector.tensor_copy(i_hi[:, i % 4, :], inter[:, i % 2, :]).then_inc(i_hi_done, 1)

            def batch(b, par, first, last):
                for i in range(STEPS):
                    n = STEPS * b + i
                    before = (i - 1) % STEPS
                    if i == 2 and not first:
                        add_ffn(b - 1)
                    maxima(n, i)
                    if not (first and i == 0):
                        twice_gelu(n - 1, before)
                    if i == 3 and not first:
                        attention_lo(b - 1)
                    if i == 5 and not first:
                        add_attention(b - 1)
                    if not last:
                        if i == 0:
                            stats(b + 1)
                        if i == 1:
                            moments(b + 1)
                        if i == 4:
                            tokens_lo(b + 1, 1 - par)
                        if i == 7:
                            latent_lo(b + 1)
                        if i == 9:
                            queries_lo(b + 1)
                        if i == 11:
                            keys_lo(b + 1)
                    if not (first and i == 0):
                        gated(n - 1, before)
                        reciprocals(n, i)
                        intermediate_hi(n - 1, before)
                    else:
                        reciprocals(n, i)
                    polynomial(n, i)
                    if first and i % 2 == 1 and (i + 3) // 2 < CHUNKS:
                        decode_chunk((i + 3) // 2)

            stats(0)
            moments(0)
            dve.wait_ge(aw_hi_done, 1)
            lo_piece(aw_lo[:, :], aw[:, :], aw_hi[:, :], UP, aw_ready)
            dve.wait_ge(const_ready, 5)
            tokens_lo(0, 0)
            latent_lo(0)
            queries_lo(0)
            decode_chunk(0)
            keys_lo(0)
            decode_chunk(1)
            batch(0, 0, True, False)
            with dve.Fori(0, (B - 2) // 2) as it:
                batch(2 * it + 1, 1, False, False)
                batch(2 * it + 2, 0, False, False)
            batch(B - 1, 1, False, True)
            end, at = STEPS * B - 1, STEPS - 1
            twice_gelu(end, at)
            gated(end, at)
            intermediate_hi(end, at)
            attention_lo(B - 1)
            add_ffn(B - 1)
            add_attention(B - 1)

        @block.tensor
        def _(pe):
            def product(out_, terms, begin=True, end=True, loose=False):
                for j, (w, m) in enumerate(terms):
                    op = nc.tensor.matmul(out_, w, m, start=begin and j == 0, stop=end and j == len(terms) - 1,
                                          skip_group_check=loose)
                return op

            def pieces(w, m):
                (wh, wl), (mh, ml) = w, m
                return [(wh, mh), (wh, ml), (wl, mh)]

            def xT(par, t):
                return xT_hi[:, par, t, :], xT_lo[:, par, t, :]

            def aws(c0, c1):
                return aw_hi[:, c0:c1], aw_lo[:, c0:c1]

            def transpose_tokens(b):
                pe.wait_ge(xn_ready, b + 1)
                if some(b):
                    pe.wait_ge(k_split, b)
                for t in range(KT):
                    for tt in range(TT):
                        op = nc.tensor.transpose(m0[:, S * t + P * tt:S * t + P * tt + P], xn[:, tt, t:D:KT], ident[:, :])
                op.then_inc(x_transposed, 1)

            def latent(b, par):
                pe.wait_ge(x_split, b + 1)
                product(m0[:, 0:S], [p for t in range(KT) for p in
                                     pieces(aws(A_WKV + P * t, A_WKV + P * t + P), xT(par, t))]).then_inc(lat_done, 1)

            def queries(b, par, tile):
                if tile == 0:
                    if some(b - 1):
                        pe.wait_ge(out_ready, b - 1)
                op = product(m1[:, S * tile:S * tile + S],
                             [p for t in range(KT) for p in
                              pieces(aws(A_WQ + D * t + P * tile, A_WQ + D * t + P * tile + P), xT(par, t))])
                if tile == 1:
                    op.then_inc(q_done, 1)

            def keys(b):
                pe.wait_ge(lat_split, b + 1)
                for tile in range(2):
                    c0 = A_WK + P * tile
                    op = product(m0[:, S * tile:S * tile + S], [(w, lat[:, :]) for w in aws(c0, c0 + P)])
                op.then_inc(k_done, 1)

            def values(b):
                pe.wait_ge(q_split, b + 1)
                for tt in range(TT):
                    op = product(m1[:, D * tt:D * tt + D], [(lat[:, P * tt:P * tt + P], w) for w in aws(A_WV, A_WO)])
                op.then_inc(v_done, 1)

            def scores(b, par, i):
                n = STEPS * b + i
                if i == 0:
                    pe.wait_ge(stack_loaded, 16 * STACK_LOADS * (b + 1))
                if some(2 * n):
                    pe.wait_ge(max_done, 2 * n)
                h = head_of(i)
                r = 64 * (h % 2)
                q, k = q_stack[r:r + 64, par, h // 2, :], k_stack[r:r + 64, par, h // 2, :]
                product(sc_ps[:, 0:P], [(q[:, 0:P], k[:, 0:P])])
                product(sc_ps[:, P:3 * P], [(q[:, P:S], k[:, 0:S])]).then_inc(scores_done, 1)

            def gate_up(b, par, i, first):
                n = STEPS * b + i
                if i == 0:
                    pe.wait_ge(x_split, b + 1)
                if first:
                    pe.wait_ge(w_ready, i // 2 + 1)
                if some(n - 1):
                    pe.wait_ge(inter_done, n - 1)
                cols = slice(P * (i % 2), P * (i % 2) + P)
                for m in (GATE, UPW):
                    op = product(gu[i % 2][:, S * m:S * m + S],
                                 [p for t in range(KT) for p in
                                  pieces((w_hi[:, i // 2, t, m, cols], w_lo[:, i // 2, t, m, cols]), xT(par, t))])
                op.then_inc(gu_done, 1)

            def transpose_probs(n, i):
                pe.wait_ge(normed, n + 1)
                if some(n):
                    pe.wait_ge(pT_stored, n)
                for c in range(3):
                    op = nc.tensor.transpose(pT_ps[:, P * c:P * c + P], probs[:, i % 2, P * c:P * c + P], ident[:, :])
                op.then_inc(pT_done, 1)

            def down(b, i):
                n = STEPS * b + i
                if i == 0:
                    if some(b):
                        pe.wait_ge(ffn_done, b)
                pe.wait_ge(i_split, n + 1)
                w = w_hi[:, i // 2, i % 2, DOWNW, :], w_lo[:, i // 2, i % 2, DOWNW, :]
                for tt in range(TT):
                    hidden = i_hi[:, i % 4, P * tt:P * tt + P], i_lo[:, i % 4, P * tt:P * tt + P]
                    op = product(acc[:, D * tt:D * tt + D], pieces(hidden, w), begin=i == 0 and tt == 0,
                                 end=i == STEPS - 1, loose=True)
                op.then_inc(down_done, 1)

            def attend(b, par, g):
                pe.wait_ge(pT_stored, STEPS * b + 4 * g + 4)
                if g == 0:
                    pe.wait_ge(v_stored, 4 * (b + 1))
                    if some(b):
                        pe.wait_ge(o_split, b)
                tile, odd = divmod(g, 2)
                for kt, (c0, c1, first_token) in enumerate(((0, S, 0), (S, 3 * P, P))):
                    for quadrant in range(4):
                        i = 4 * g + quadrant
                        r = 32 * quadrant
                        op = nc.tensor.matmul(o_ps[r:r + 32, S * tile + first_token:S * tile + S],
                                              v_pad[:, par, kt, head_of(i), :], pT[:, i % 8, c0:c1],
                                              start=odd == 0 and kt == 0, stop=odd == 1 and kt == 1, skip_group_check=True)
                op.then_inc(pv_done, 1)

            def project(b, batches):
                pe.wait_ge(o_split, b + 1)
                pe.wait_ge(v_stored, 4 * batches)
                for tt in range(TT):
                    tokens = slice(P * tt, P * tt + P)
                    op = product(m1[:, D * tt:D * tt + D],
                                 [p for t in range(2) for p in
                                  pieces((o_hi[:, t, tokens], o_lo[:, t, tokens]), aws(A_WO + D * t, A_WO + D * t + D))])
                op.then_inc(wo_done, 1)

            def batch(b, par, first, last):
                for i in range(STEPS):
                    n = STEPS * b + i
                    scores(b, par, i)
                    gate_up(b, par, i, first)
                    if not (first and i == 0):
                        transpose_probs(n - 1, (i - 1) % STEPS)
                    if i >= 2:
                        down(b, i - 2)
                    elif not first:
                        down(b - 1, STEPS - 2 + i)
                    if i == 1 and not first:
                        attend(b - 1, 1 - par, GROUPS - 1)
                    if i in (5, 9, 13):
                        attend(b, par, i // 4 - 1)
                    if i == 4 and not first:
                        project(b - 1, b + 1)
                    if not last:
                        if i == 3:
                            transpose_tokens(b + 1)
                        if i == 6:
                            latent(b + 1, 1 - par)
                        if i in (7, 8):
                            queries(b + 1, 1 - par, i - 7)
                        if i == 10:
                            keys(b + 1)
                        if i == 11:
                            values(b + 1)

            pe.wait_ge(const_ready, 5)
            transpose_tokens(0)
            pe.wait_ge(aw_ready, 1)
            latent(0, 0)
            queries(0, 0, 0)
            queries(0, 0, 1)
            keys(0)
            values(0)
            batch(0, 0, True, False)
            with pe.Fori(0, (B - 2) // 2) as it:
                batch(2 * it + 1, 1, False, False)
                batch(2 * it + 2, 0, False, False)
            batch(B - 1, 1, False, True)
            transpose_probs(STEPS * B - 1, STEPS - 1)
            down(B - 1, STEPS - 2)
            attend(B - 1, 1, GROUPS - 1)
            down(B - 1, STEPS - 1)
            project(B - 1, B)


def kernel(**inputs):
    import numpy as _np
    import concourse.bacc as _bacc
    from concourse.bass_utils import run_bass_kernel_spmd as _run

    a = {k.removeprefix("L0_"): _np.asarray(v) for k, v in inputs.items()}
    def by_byte(w):
        return w.reshape(CHUNKS, P, 2, -1).transpose(3, 0, 2, 1).reshape(-1, CHUNKS, 2 * P)

    def by_unit(w):
        return w.T.reshape(CHUNKS, -1, D).transpose(1, 0, 2)

    packed = _np.stack([by_byte(a["ffn_gate_W_packed"]), by_byte(a["ffn_up_W_packed"]), by_unit(a["ffn_down_W_packed"])], axis=2)
    scales = _np.stack([by_byte(a["ffn_gate_scales"]), by_byte(a["ffn_up_scales"]), by_unit(a["ffn_down_scales"])], axis=2)
    arrays = {
        "x": a["attn_x"], "wq": a["attn_Wq"], "wkv": a["attn_Wkv"], "wk": a["attn_Wk"], "wv": a["attn_Wv"], "wo": a["attn_Wo"],
        "packed": packed.reshape(P, CHUNKS, 3 * S), "scales": scales.reshape(P // 16, CHUNKS, 3 * S),
    }
    arrays = {k: _np.ascontiguousarray(v) for k, v in arrays.items()}
    nc = _bacc.Bacc("TRN2", target_bir_lowering=False, num_devices=1)
    aps = [nc.dram_tensor(k, v.shape, mybir.dt.from_np(v.dtype), kind="ExternalInput").ap() for k, v in arrays.items()]
    out = nc.dram_tensor("out", (B, S, D), F32, kind="ExternalOutput").ap()
    layer(nc, *aps, out)
    return _run(nc, [arrays], core_ids=[0]).results[0]["out"]
```

```python
import numpy as np

import concourse.bass as bass
import concourse.mybir as mybir
from concourse.alu_op_type import AluOpType as ALU
from contextlib import ExitStack

ACT = mybir.ActivationFunctionType
F32, F16, U16, I32 = mybir.dt.float32, mybir.dt.float16, mybir.dt.uint16, mybir.dt.int32

P = 128
B, S, D = 16, 256, 256
H, HD = 16, 16
L = 64
WINDOW, PERSIST = 128, 16
MLP, BLOCK = 2048, 32
TT = S // P
KT = D // P
STEPS = 16
CHUNKS = MLP // (2 * P)
IN_FLIGHT = 4
GROUPS = 4
EPS = 1e-5
UP = 256.0
DOWN = 1.0 / UP
MASKED = -1e30
GELU_CUBE = 0.044715
GELU_SLOPE = 0.7978845608028654
GATE, UPW, DOWNW = range(3)


def head_of(step):
    group, quadrant = divmod(step, 4)
    return 8 * (group // 2) + 2 * quadrant + group % 2


def some(count):
    return not isinstance(count, int) or count > 0


def layer(nc, x, wq, wkv, wk, wv, wo, packed, scales, out):
    ctx = ExitStack()
    with ctx:
        def sb(name, shape, dtype=F32):
            return ctx.enter_context(nc.sbuf_tensor(name, shape, dtype))

        def bank(name):
            return ctx.enter_context(nc.psum_tensor(name, [P, 512], F32))

        def sem(name):
            return ctx.enter_context(nc.semaphore(name))

        ident = sb("ident", [P, P])
        mask = sb("mask", [P, 3 * P])
        x_in = sb("x_in", [P, TT, D])
        x_res = sb("x_res", [P, TT, D])
        bn = sb("bn", [P, TT, 6])
        mv = sb("mv", [P, TT, 2])
        nm = sb("nm", [P, TT])
        ve = sb("ve", [P, TT])
        minus_half = sb("minus_half", [P, TT])
        rstd = sb("rstd", [P, TT])
        xn = sb("xn", [P, TT, D])
        xT_hi = sb("xT_hi", [P, 2, KT, S], F16)
        xT_lo = sb("xT_lo", [P, 2, KT, S], F16)
        A_WQ, A_WKV, A_WK, A_WV, A_WO, A_END = 0, 512, 768, 1024, 1280, 1792
        aw = sb("aw", [P, A_END])
        aw_hi = sb("aw_hi", [P, A_END], F16)
        aw_lo = sb("aw_lo", [P, A_END], F16)
        lat = sb("lat", [P, S], F16)
        q_hi = sb("q_hi", [P, 2, S], F16)
        q_lo = sb("q_lo", [P, 2, S], F16)
        k_hi = sb("k_hi", [P, 2, S], F16)
        k_lo = sb("k_lo", [P, 2, S], F16)
        q_stack = sb("q_stack", [P, 2, H // 4, 2 * S], F16)
        k_stack = sb("k_stack", [P, 2, H // 4, 2 * S], F16)
        v_pad = sb("v_pad", [P, 2, TT, H, 2 * HD])
        s_neg = sb("s_neg", [P, 2, 3 * P])
        nmax = sb("nmax", [P, 2, TT])
        probs = sb("probs", [P, 2, 3 * P])
        rowsum = sb("rowsum", [P, 2, TT])
        rrow = sb("rrow", [P, 2, TT])
        pT = sb("pT", [P, 8, 3 * P])
        o_hi = sb("o_hi", [P, 2, S], F16)
        o_lo = sb("o_lo", [P, 2, S], F16)
        sq = sb("sq", [P, 2, S])
        poly = sb("poly", [P, 2, S])
        th = sb("th", [P, 2, S])
        gelu = sb("gelu", [P, 2, S])
        inter = sb("inter", [P, 2, S])
        i_hi = sb("i_hi", [P, 4, S], F16)
        i_lo = sb("i_lo", [P, 4, S], F16)
        ffn = sb("ffn", [P, TT * D])
        o_sb = sb("o_sb", [P, TT * D])
        pk = sb("pk", [P, IN_FLIGHT, 3 * S], I32)
        sc = sb("sc", [P, IN_FLIGHT, 3 * S])
        code = sb("code", [P, 2, 3 * S], U16)
        sign = sb("sign", [P, 2, 3 * S], U16)
        low = sb("low", [P, 2, 3 * S], F16)
        wf = sb("wf", [P, 2, 2, 3 * S])
        w_hi = sb("w_hi", [P, CHUNKS, 2, 3, S], F16)
        w_lo = sb("w_lo", [P, CHUNKS, 2, 3, S], F16)
        q_dram = nc.dram_tensor("q_rows", [2, H // 2, 4, HD, 2 * S], F16, kind="Internal").ap()
        k_dram = nc.dram_tensor("k_rows", [2, H // 2, 4, HD, 2 * S], F16, kind="Internal").ap()

        gu = [bank("gu0"), bank("gu1")]
        acc = bank("acc")
        sc_ps = bank("sc_ps")
        pT_ps = bank("pT_ps")
        o_ps = bank("o_ps")
        m0 = bank("m0")
        m1 = bank("m1")

        aw_loaded, aw_hi_done, aw_ready = [sem("aw_loaded0"), sem("aw_loaded1")], sem("aw_hi_done"), sem("aw_ready")
        pk_loaded = [sem(f"pk_loaded{c}") for c in range(CHUNKS)]
        decode = sem("decode")
        w_float, w_hi_done, w_ready = sem("w_float"), sem("w_hi_done"), sem("w_ready")
        const_step, const_ready = sem("const_step"), sem("const_ready")
        passed = sem("passed")
        x_loaded, res_loaded = sem("x_loaded"), sem("res_loaded")
        bn_done, aggr_done, stats_ready = sem("bn_done"), sem("aggr_done"), sem("stats_ready")
        rstd_done, xn_ready = sem("rstd_done"), sem("xn_ready")
        x_transposed, x_hi_done, x_split = sem("x_transposed"), sem("x_hi_done"), sem("x_split")
        lat_done, lat_hi_done, lat_split = sem("lat_done"), sem("lat_hi_done"), sem("lat_split")
        q_done, q_hi_done, q_split = sem("q_done"), sem("q_hi_done"), sem("q_split")
        k_done, k_hi_done, k_split = sem("k_done"), sem("k_hi_done"), sem("k_split")
        v_done, v_stored = sem("v_done"), sem("v_stored")
        q_rows_stored, k_rows_stored = sem("q_rows_stored"), sem("k_rows_stored")
        q_loaded, k_loaded = sem("q_loaded"), sem("k_loaded")
        scores_done, max_done, exp_done = sem("scores_done"), sem("max_done"), sem("exp_done")
        recip_done, normed = sem("recip_done"), sem("normed")
        pT_done, pT_stored, pv_done = sem("pT_done"), sem("pT_stored"), sem("pv_done")
        o_hi_done, o_split, wo_done = sem("o_hi_done"), sem("o_split"), sem("wo_done")
        gu_done, sq_done, poly_done = sem("gu_done"), sem("sq_done"), sem("poly_done")
        th_done, gelu_done, inter_done = sem("th_done"), sem("gelu_done"), sem("inter_done")
        i_hi_done, i_split, down_done = sem("i_hi_done"), sem("i_split"), sem("down_done")
        ffn_done, out_ready, out_stored = sem("ffn_done"), sem("out_ready"), sem("out_stored")

        def alone(eng):
            eng.sem_inc(passed, 1)

        x_tok = x.rearrange("b (t p) d -> b p t d", p=P)
        out_tok = out.rearrange("b (t p) d -> b p t d", p=P)
        ROW_STORES = 4

        block = ctx.enter_context(nc.Block())

        @block.sync
        def _(sp):
            def load_tokens(b):
                sp.dma_start(x_in[:, :, :], x_tok[b]).then_inc(x_loaded, 16)

            def store_rows(b, par):
                sp.wait_ge(q_split, b + 1)
                for piece, src in enumerate((q_hi, q_lo, q_hi, q_lo)):
                    sp.dma_start(q_dram[par, :, piece], src[:, :, :].rearrange("p t s -> p (t s)")).then_inc(q_rows_stored, 16)
                sp.wait_ge(k_split, b + 1)
                for piece, src in enumerate((k_hi, k_lo, k_lo, k_hi)):
                    sp.dma_start(k_dram[par, :, piece], src[:, :, :].rearrange("p t s -> p (t s)")).then_inc(k_rows_stored, 16)

            def load_stacks(b, par):
                sp.wait_ge(q_rows_stored, 16 * ROW_STORES * (b + 1))
                sp.dma_start(q_stack[:, par, :, :], q_dram[par].rearrange("(g o) c d n -> (o c d) g n", o=2)).then_inc(q_loaded, 16)
                sp.wait_ge(k_rows_stored, 16 * ROW_STORES * (b + 1))
                sp.dma_start(k_stack[:, par, :, :], k_dram[par].rearrange("(g o) c d n -> (o c d) g n", o=2)).then_inc(k_loaded, 16)

            def batch(b, par, first, last):
                if not (first or last):
                    sp.wait_ge(xn_ready, TT * (b + 1))
                    alone(sp)
                    load_tokens(b + 1)
                if some(b):
                    sp.wait_ge(ffn_done, b)
                alone(sp)
                sp.dma_start(x_res[:, :, :], x_tok[b]).then_inc(res_loaded, 16)
                if not first:
                    if some(b):
                        sp.wait_ge(out_ready, b)
                    alone(sp)
                    sp.dma_start(out_tok[b - 1], o_sb[:, :].rearrange("p (t d) -> p t d", t=TT)).then_inc(out_stored, 16)
                if not last:
                    store_rows(b + 1, 1 - par)
                    if some(STEPS * b):
                        sp.wait_ge(scores_done, STEPS * b)
                    alone(sp)
                    load_stacks(b + 1, 1 - par)

            load_tokens(0)
            sp.dma_start(aw[:, A_WKV:A_WK].rearrange("p (t c n) -> p t c n", t=KT, c=2),
                         wkv.rearrange("(p t c) n -> p t c n", t=KT, c=1).to_broadcast([P, KT, 2, L])).then_inc(aw_loaded[0], 16)
            sp.dma_start(aw[:, A_WQ:A_WKV].rearrange("p (t n) -> p t n", t=KT),
                         wq.rearrange("(p t) n -> p t n", t=KT)).then_inc(aw_loaded[0], 16)

            def load_chunk(c):
                if some(c - IN_FLIGHT + 1):
                    sp.wait_ge(w_float, c - IN_FLIGHT + 1)
                sp.dma_start(pk[:, c % IN_FLIGHT, :], packed[:, c, :]).then_inc(pk_loaded[c], 16)
                sp.dma_start(sc[:, c % IN_FLIGHT, :],
                             scales[:, c:c + 1, :].to_broadcast([P // 16, 16, 3 * S])).then_inc(pk_loaded[c], 16)

            load_chunk(0)
            for c0, w in ((A_WK, wk), (A_WV, wv)):
                sp.dma_start(aw[:, c0:c0 + D], w.rearrange("(c l) n -> c l n", c=1).to_broadcast([2, L, D])).then_inc(aw_loaded[1], 16)
            sp.dma_start(aw[:, A_WO:A_END].rearrange("p (t n) -> p t n", t=2),
                         wo.rearrange("(t p) n -> p t n", t=2)).then_inc(aw_loaded[1], 16)
            for c in range(1, IN_FLIGHT):
                load_chunk(c)
            sp.wait_ge(xn_ready, TT)
            load_tokens(1)
            store_rows(0, 0)
            load_stacks(0, 0)
            for c in range(IN_FLIGHT, CHUNKS):
                load_chunk(c)
            batch(0, 0, True, False)
            with sp.Fori(0, (B - 2) // 2) as it:
                batch(2 * it + 1, 1, False, False)
                batch(2 * it + 2, 0, False, False)
            batch(B - 1, 1, False, True)
            sp.wait_ge(out_ready, B)
            sp.dma_start(out_tok[B - 1], o_sb[:, :].rearrange("p (t d) -> p t d", t=TT)).then_inc(out_stored, 16)
            sp.wait_ge(out_stored, 16 * B)

        @block.gpsimd
        def _(pool):
            def weights_lo(c):
                pool.wait_ge(w_hi_done, c + 1)
                nc.gpsimd.tensor_tensor(w_lo[:, c].rearrange("p a m n -> p (a m n)"),
                                        wf[:, c % 2].rearrange("p a n -> p (a n)"),
                                        w_hi[:, c].rearrange("p a m n -> p (a m n)"), ALU.subtract).then_inc(w_ready, 1)

            def inverse_deviation(b):
                pool.wait_ge(stats_ready, 2 * (b + 1))
                nc.gpsimd.tensor_tensor(rstd[:, :], ve[:, :], minus_half[:, :], ALU.pow).then_inc(rstd_done, 1)

            def norm_tokens(b, t):
                pool.wait_ge(rstd_done, b + 1)
                if some(b):
                    pool.wait_ge(x_transposed, b)
                alone(pool)
                nc.gpsimd.tensor_scalar(xn[:, t, :], x_in[:, t, :], nm[:, t:t + 1], rstd[:, t:t + 1],
                                        ALU.add, ALU.mult).then_inc(xn_ready, 1)

            def intermediate_lo(n, i):
                pool.wait_ge(i_hi_done, n + 1)
                nc.gpsimd.tensor_tensor(i_lo[:, i % 4, :], inter[:, i % 2, :], i_hi[:, i % 4, :],
                                        ALU.subtract).then_inc(i_split, 1)

            def scale_probs(n, i):
                pool.wait_ge(recip_done, n + 1)
                alone(pool)
                r = i % 2
                nc.gpsimd.tensor_scalar(probs[:, r, 0:P], probs[:, r, 0:P], rrow[:, r, 0:1], 1.0, ALU.mult, ALU.mult)
                nc.gpsimd.tensor_scalar(probs[:, r, P:3 * P], probs[:, r, P:3 * P], rrow[:, r, 1:2], 1.0,
                                        ALU.mult, ALU.mult).then_inc(normed, 1)

            def batch(b, par, first, last):
                for i in range(STEPS):
                    n = STEPS * b + i
                    if not (first and i == 0):
                        intermediate_lo(n - 1, (i - 1) % STEPS)
                    scale_probs(n, i)
                    if i == 1 and not last:
                        inverse_deviation(b + 1)
                        norm_tokens(b + 1, 0)
                    if i == 2 and not last:
                        norm_tokens(b + 1, 1)
                    if first and i % 2 == 1 and (i + 3) // 2 < CHUNKS:
                        weights_lo((i + 3) // 2)

            nc.gpsimd.memset(ident[:, :], 0.0).then_inc(const_step, 1)
            nc.gpsimd.memset(mask[:, :], 0.0).then_inc(const_step, 1)
            nc.gpsimd.memset(minus_half[:, :], -0.5).then_inc(const_step, 1)
            nc.gpsimd.memset(v_pad[:, :, :, :, :], 0.0).then_inc(const_ready, 1)
            pool.wait_ge(const_step, 3)
            nc.gpsimd.affine_select(out=ident[:, :], in_=ident[:, :], compare_op=ALU.not_equal, fill=1.0, base=0,
                                    pattern=[[-1, P]], channel_multiplier=1).then_inc(const_ready, 1)
            for c0 in (0, 2 * P):
                nc.gpsimd.affine_select(out=mask[:, c0:c0 + P], in_=mask[:, c0:c0 + P], compare_op=ALU.is_ge,
                                        fill=MASKED, base=0, pattern=[[-1, P]], channel_multiplier=1).then_inc(const_ready, 1)
            nc.gpsimd.affine_select(out=mask[:, P + PERSIST:2 * P], in_=mask[:, P + PERSIST:2 * P], compare_op=ALU.is_ge,
                                    fill=MASKED, base=PERSIST - (P - WINDOW) - 1, pattern=[[1, P - PERSIST]],
                                    channel_multiplier=-1).then_inc(const_ready, 1)
            inverse_deviation(0)
            norm_tokens(0, 0)
            norm_tokens(0, 1)
            weights_lo(0)
            weights_lo(1)
            batch(0, 0, True, False)
            with pool.Fori(0, (B - 2) // 2) as it:
                batch(2 * it + 1, 1, False, False)
                batch(2 * it + 2, 0, False, False)
            batch(B - 1, 1, False, True)
            intermediate_lo(STEPS * B - 1, STEPS - 1)

        @block.scalar
        def _(act):
            def hi_piece(dst, src, scale, done):
                nc.scalar.activation(dst, src, ACT.Copy, scale=scale).then_inc(done, 1)

            def weights_hi(c):
                act.wait_ge(w_float, c + 1)
                hi_piece(w_hi[:, c].rearrange("p a m n -> p (a m n)"), wf[:, c % 2].rearrange("p a n -> p (a n)"), 1.0, w_hi_done)

            def tokens_hi(b, par):
                act.wait_ge(x_transposed, b + 1)
                hi_piece(xT_hi[:, par], m0[:, :].rearrange("p (t s) -> p t s", t=KT), 1.0, x_hi_done)

            def latent_hi(b):
                if some(b):
                    act.wait_ge(v_done, b)
                act.wait_ge(lat_done, b + 1)
                hi_piece(lat[:, :], m0[:, 0:S], DOWN, lat_hi_done)

            def queries_hi(b):
                if some(16 * ROW_STORES * b):
                    act.wait_ge(q_rows_stored, 16 * ROW_STORES * b)
                act.wait_ge(q_done, b + 1)
                hi_piece(q_hi[:, :, :], m1[:, :].rearrange("p (t s) -> p t s", t=2), DOWN, q_hi_done)

            def keys_hi(b):
                if some(16 * ROW_STORES * b):
                    act.wait_ge(k_rows_stored, 16 * ROW_STORES * b)
                act.wait_ge(k_done, b + 1)
                hi_piece(k_hi[:, :, :], m0[:, :].rearrange("p (t s) -> p t s", t=2), DOWN, k_hi_done)

            def values_store(b, par, t):
                act.wait_ge(v_done, b + 1)
                if some(GROUPS * (b - 1)):
                    act.wait_ge(pv_done, GROUPS * (b - 1))
                for odd in range(2):
                    dst = v_pad[:, par, t, odd:H:2, HD * odd:HD * odd + HD]
                    src = m1[:, D * t:D * t + D].rearrange("p (h d) -> p h d", d=HD)[:, odd:H:2, :]
                    hi_piece(dst, src, DOWN, v_stored)

            def attention_hi(b):
                if some(b):
                    act.wait_ge(wo_done, b)
                act.wait_ge(pv_done, GROUPS * (b + 1))
                hi_piece(o_hi[:, :, :], o_ps[:, :].rearrange("p (t s) -> p t s", t=2), 1.0, o_hi_done)

            def exponentials(n, i):
                if some(n - 1):
                    act.wait_ge(pT_done, n - 1)
                act.wait_ge(max_done, 2 * (n + 1))
                r = i % 2
                nc.scalar.activation(probs[:, r, 0:P], s_neg[:, r, 0:P], ACT.Exp, bias=nmax[:, r, 0:1], scale=-1.0,
                                     accum_out=rowsum[:, r, 0:1])
                nc.scalar.activation(probs[:, r, P:3 * P], s_neg[:, r, P:3 * P], ACT.Exp, bias=nmax[:, r, 1:2], scale=-1.0,
                                     accum_out=rowsum[:, r, 1:2]).then_inc(exp_done, 1)

            def squares(n, i):
                act.wait_ge(gu_done, n + 1)
                nc.scalar.activation(sq[:, i % 2, :], gu[i % 2][:, 0:S], ACT.Square,
                                     scale=GELU_CUBE ** 0.5 * DOWN).then_inc(sq_done, 1)

            def tanhs(n, i):
                act.wait_ge(poly_done, n + 1)
                nc.scalar.activation(th[:, i % 2, :], poly[:, i % 2, :], ACT.Tanh, scale=GELU_SLOPE * DOWN).then_inc(th_done, 1)

            def store_pT(b, i):
                n = STEPS * b + i
                if i % 4 == 0:
                    if some(GROUPS * b + i // 4 - 1):
                        act.wait_ge(pv_done, GROUPS * b + i // 4 - 1)
                act.wait_ge(pT_done, n + 1)
                nc.scalar.activation(pT[:, i % 8, :], pT_ps[:, 0:3 * P], ACT.Copy).then_inc(pT_stored, 1)

            def batch(b, par, first, last):
                for i in range(STEPS):
                    n = STEPS * b + i
                    exponentials(n, i)
                    squares(n, i)
                    if not (first and i == 0):
                        if i == 0:
                            store_pT(b - 1, STEPS - 1)
                        else:
                            store_pT(b, i - 1)
                    if i == 2 and not first:
                        attention_hi(b - 1)
                    if not last:
                        if i == 3:
                            tokens_hi(b + 1, 1 - par)
                        if i == 6:
                            latent_hi(b + 1)
                        if i == 8:
                            queries_hi(b + 1)
                        if i == 10:
                            keys_hi(b + 1)
                        if i in (11, 12):
                            values_store(b + 1, 1 - par, i - 11)
                    tanhs(n, i)
                    if first and i % 2 == 1 and (i + 3) // 2 < CHUNKS:
                        weights_hi((i + 3) // 2)

            def weights_of_attention(part, loads, c0, c1):
                act.wait_ge(aw_loaded[part], 16 * loads)
                hi_piece(aw_hi[:, c0:c1], aw[:, c0:c1], UP, aw_hi_done)

            weights_of_attention(0, 2, 0, A_WK)
            act.wait_ge(const_ready, 5)
            tokens_hi(0, 0)
            weights_of_attention(1, 3, A_WK, A_END)
            latent_hi(0)
            queries_hi(0)
            keys_hi(0)
            weights_hi(0)
            values_store(0, 0, 0)
            values_store(0, 0, 1)
            weights_hi(1)
            batch(0, 0, True, False)
            with act.Fori(0, (B - 2) // 2) as it:
                batch(2 * it + 1, 1, False, False)
                batch(2 * it + 2, 0, False, False)
            batch(B - 1, 1, False, True)
            store_pT(B - 1, STEPS - 1)
            attention_hi(B - 1)

        @block.vector
        def _(dve):
            decoded = [0]

            def link(op):
                decoded[0] += 1
                op.then_inc(decode, 1)
                dve.wait_ge(decode, decoded[0])

            def decode_codes(c):
                dve.wait_ge(pk_loaded[c], 16 * 2)
                byte = pk[:, c % IN_FLIGHT, :].bitcast(U16).rearrange("p (n two) -> p n two", two=2)[:, :, 0]
                for nibble, shift in ((0, 9), (1, 5)):
                    op = nc.vector.tensor_scalar(code[:, nibble, :], byte, shift, 0x1E00, ALU.logical_shift_left, ALU.bitwise_and)
                link(op)
                code_all = code[:, :, :].rearrange("p a n -> p (a n)")
                sign_all = sign[:, :, :].rearrange("p a n -> p (a n)")
                nc.vector.tensor_scalar(sign_all, code_all, 0x1000, 3, ALU.bitwise_and, ALU.logical_shift_left)
                link(nc.vector.tensor_scalar(code_all, code_all, 0x0E00, 0x4000, ALU.bitwise_and, ALU.bitwise_or))

            def decode_values(c):
                code_all = code[:, :, :].rearrange("p a n -> p (a n)")
                sign_all = sign[:, :, :].rearrange("p a n -> p (a n)")
                low_all = low[:, :, :].rearrange("p a n -> p (a n)")
                link(nc.vector.tensor_scalar(low_all, code_all.bitcast(F16), -4.0, 0.0, ALU.add, ALU.min))
                link(nc.vector.tensor_tensor(low_all, low_all, code_all.bitcast(F16), ALU.add))
                link(nc.vector.tensor_tensor(sign_all, sign_all, low_all.bitcast(U16), ALU.bitwise_xor))

            def decode_scale(c):
                if some(c - 1):
                    dve.wait_ge(w_ready, c - 1)
                nc.vector.scalar_tensor_tensor(out=wf[:, c % 2], in0=sign[:, :, :].bitcast(F16), scalar=UP / 4.0,
                                               in1=sc[:, c % IN_FLIGHT:c % IN_FLIGHT + 1, :].to_broadcast([P, 2, 3 * S]),
                                               op0=ALU.mult, op1=ALU.mult).then_inc(w_float, 1)

            def lo_piece(dst, src, hi, scale, done):
                nc.vector.scalar_tensor_tensor(out=dst, in0=src, scalar=scale, in1=hi,
                                               op0=ALU.mult, op1=ALU.subtract).then_inc(done, 1)

            def stats(b):
                dve.wait_ge(x_loaded, 16 * (b + 1))
                for t in range(TT):
                    op = nc.vector.bn_stats(bn[:, t, :], x_in[:, t, :])
                op.then_inc(bn_done, 1)

            def moments(b):
                dve.wait_ge(bn_done, b + 1)
                alone(dve)
                for t in range(TT):
                    op = nc.vector.bn_aggr(mv[:, t, :], bn[:, t, :])
                op.then_inc(aggr_done, 1)
                dve.wait_ge(aggr_done, b + 1)
                nc.vector.tensor_scalar(nm[:, :], mv[:, :, 0], -1.0, None, ALU.mult).then_inc(stats_ready, 1)
                nc.vector.tensor_scalar(ve[:, :], mv[:, :, 1], EPS, None, ALU.add).then_inc(stats_ready, 1)

            def tokens_lo(b, par):
                dve.wait_ge(x_hi_done, b + 1)
                lo_piece(xT_lo[:, par], m0[:, :].rearrange("p (t s) -> p t s", t=KT), xT_hi[:, par], 1.0, x_split)

            def latent_lo(b):
                dve.wait_ge(lat_hi_done, b + 1)
                lo_piece(lat[L:P, :], m0[L:P, 0:S], lat[L:P, :], DOWN, lat_split)

            def queries_lo(b):
                dve.wait_ge(q_hi_done, b + 1)
                lo_piece(q_lo[:, :, :], m1[:, :].rearrange("p (t s) -> p t s", t=2), q_hi[:, :, :], DOWN, q_split)

            def keys_lo(b):
                dve.wait_ge(k_hi_done, b + 1)
                lo_piece(k_lo[:, :, :], m0[:, :].rearrange("p (t s) -> p t s", t=2), k_hi[:, :, :], DOWN, k_split)

            def attention_lo(b):
                dve.wait_ge(o_hi_done, b + 1)
                lo_piece(o_lo[:, :, :], o_ps[:, :].rearrange("p (t s) -> p t s", t=2), o_hi[:, :, :], 1.0, o_split)

            def add_ffn(b):
                dve.wait_ge(down_done, STEPS * (b + 1))
                dve.wait_ge(res_loaded, 16 * (b + 1))
                nc.vector.scalar_tensor_tensor(out=ffn[:, :], in0=acc[:, :], scalar=DOWN,
                                               in1=x_res[:, :, :].rearrange("p t d -> p (t d)"),
                                               op0=ALU.mult, op1=ALU.add).then_inc(ffn_done, 1)

            def add_attention(b):
                if some(16 * b):
                    dve.wait_ge(out_stored, 16 * b)
                dve.wait_ge(wo_done, b + 1)
                dve.wait_ge(ffn_done, b + 1)
                nc.vector.scalar_tensor_tensor(out=o_sb[:, :], in0=m1[:, :], scalar=DOWN, in1=ffn[:, :],
                                               op0=ALU.mult, op1=ALU.add).then_inc(out_ready, 1)

            def maxima(n, i):
                if some(n - 1):
                    dve.wait_ge(exp_done, n - 1)
                dve.wait_ge(scores_done, n + 1)
                alone(dve)
                r = i % 2
                for t, (c0, c1) in enumerate(((0, P), (P, 3 * P))):
                    nc.vector.tensor_tensor_reduce(out=s_neg[:, r, c0:c1], in0=sc_ps[:, c0:c1], in1=mask[:, c0:c1],
                                                   scale=-1.0 / HD ** 0.5, scalar=3e38, op0=ALU.add, op1=ALU.min,
                                                   accum_out=nmax[:, r, t:t + 1]).then_inc(max_done, 1)

            def reciprocals(n, i):
                dve.wait_ge(exp_done, n + 1)
                nc.vector.reciprocal(rrow[:, i % 2, :], rowsum[:, i % 2, :]).then_inc(recip_done, 1)

            def polynomial(n, i):
                dve.wait_ge(sq_done, n + 1)
                nc.vector.scalar_tensor_tensor(out=poly[:, i % 2, :], in0=sq[:, i % 2, :], scalar=1.0,
                                               in1=gu[i % 2][:, 0:S], op0=ALU.add, op1=ALU.mult).then_inc(poly_done, 1)

            def twice_gelu(n, i):
                dve.wait_ge(th_done, n + 1)
                nc.vector.scalar_tensor_tensor(out=gelu[:, i % 2, :], in0=th[:, i % 2, :], scalar=1.0,
                                               in1=gu[i % 2][:, 0:S], op0=ALU.add, op1=ALU.mult).then_inc(gelu_done, 1)

            def gated(n, i):
                if some(n - 1):
                    dve.wait_ge(i_split, n - 1)
                dve.wait_ge(gelu_done, n + 1)
                nc.vector.scalar_tensor_tensor(out=inter[:, i % 2, :], in0=gelu[:, i % 2, :], scalar=0.5 * DOWN * DOWN,
                                               in1=gu[i % 2][:, S:2 * S], op0=ALU.mult, op1=ALU.mult).then_inc(inter_done, 1)

            def intermediate_hi(n, i):
                if some(n - 3):
                    dve.wait_ge(down_done, n - 3)
                dve.wait_ge(inter_done, n + 1)
                nc.vector.tensor_copy(i_hi[:, i % 4, :], inter[:, i % 2, :]).then_inc(i_hi_done, 1)

            def batch(b, par, first, last):
                for i in range(STEPS):
                    n = STEPS * b + i
                    before = (i - 1) % STEPS
                    if i == 2 and not first:
                        add_ffn(b - 1)
                    maxima(n, i)
                    if first and i % 2 == 0 and i // 2 + 2 < CHUNKS:
                        decode_codes(i // 2 + 2)
                    if not (first and i == 0):
                        twice_gelu(n - 1, before)
                    if i == 3 and not first:
                        attention_lo(b - 1)
                    if i == 5 and not first:
                        add_attention(b - 1)
                    if not last:
                        if i == 0:
                            stats(b + 1)
                        if i == 1:
                            moments(b + 1)
                        if i == 4:
                            tokens_lo(b + 1, 1 - par)
                        if i == 7:
                            latent_lo(b + 1)
                        if i == 9:
                            queries_lo(b + 1)
                        if i == 11:
                            keys_lo(b + 1)
                    if not (first and i == 0):
                        gated(n - 1, before)
                        reciprocals(n, i)
                        intermediate_hi(n - 1, before)
                    else:
                        reciprocals(n, i)
                    polynomial(n, i)
                    if first and i % 2 == 0 and i // 2 + 2 < CHUNKS:
                        decode_values(i // 2 + 2)
                    if first and i % 2 == 1 and i // 2 + 2 < CHUNKS:
                        decode_scale(i // 2 + 2)

            stats(0)
            moments(0)
            def weights_of_attention(part, c0, c1):
                dve.wait_ge(aw_hi_done, part + 1)
                lo_piece(aw_lo[:, c0:c1], aw[:, c0:c1], aw_hi[:, c0:c1], UP, aw_ready)

            weights_of_attention(0, 0, A_WK)
            decode_codes(0)
            dve.wait_ge(const_ready, 5)
            tokens_lo(0, 0)
            weights_of_attention(1, A_WK, A_END)
            latent_lo(0)
            decode_values(0)
            queries_lo(0)
            keys_lo(0)
            decode_scale(0)
            decode_codes(1)
            decode_values(1)
            decode_scale(1)
            batch(0, 0, True, False)
            with dve.Fori(0, (B - 2) // 2) as it:
                batch(2 * it + 1, 1, False, False)
                batch(2 * it + 2, 0, False, False)
            batch(B - 1, 1, False, True)
            end, at = STEPS * B - 1, STEPS - 1
            twice_gelu(end, at)
            gated(end, at)
            intermediate_hi(end, at)
            attention_lo(B - 1)
            add_ffn(B - 1)
            add_attention(B - 1)

        @block.tensor
        def _(pe):
            def product(out_, terms, begin=True, end=True, loose=False):
                for j, (w, m) in enumerate(terms):
                    op = nc.tensor.matmul(out_, w, m, start=begin and j == 0, stop=end and j == len(terms) - 1,
                                          skip_group_check=loose)
                return op

            def pieces(w, m):
                (wh, wl), (mh, ml) = w, m
                return [(wh, mh), (wh, ml), (wl, mh)]

            def xT(par, t):
                return xT_hi[:, par, t, :], xT_lo[:, par, t, :]

            def aws(c0, c1):
                return aw_hi[:, c0:c1], aw_lo[:, c0:c1]

            def transpose_tokens(b):
                pe.wait_ge(xn_ready, TT * (b + 1))
                if some(b):
                    pe.wait_ge(k_split, b)
                for t in range(KT):
                    for tt in range(TT):
                        op = nc.tensor.transpose(m0[:, S * t + P * tt:S * t + P * tt + P], xn[:, tt, t:D:KT], ident[:, :])
                op.then_inc(x_transposed, 1)

            def latent(b, par):
                pe.wait_ge(x_split, b + 1)
                product(m0[:, 0:S], [p for t in range(KT) for p in
                                     pieces(aws(A_WKV + P * t, A_WKV + P * t + P), xT(par, t))]).then_inc(lat_done, 1)

            def queries(b, par, tile):
                if tile == 0:
                    if some(b - 1):
                        pe.wait_ge(out_ready, b - 1)
                op = product(m1[:, S * tile:S * tile + S],
                             [p for t in range(KT) for p in
                              pieces(aws(A_WQ + D * t + P * tile, A_WQ + D * t + P * tile + P), xT(par, t))])
                if tile == 1:
                    op.then_inc(q_done, 1)

            def keys(b):
                pe.wait_ge(lat_split, b + 1)
                for tile in range(2):
                    c0 = A_WK + P * tile
                    op = product(m0[:, S * tile:S * tile + S], [(w, lat[:, :]) for w in aws(c0, c0 + P)])
                op.then_inc(k_done, 1)

            def values(b):
                pe.wait_ge(q_split, b + 1)
                for tt in range(TT):
                    op = product(m1[:, D * tt:D * tt + D], [(lat[:, P * tt:P * tt + P], w) for w in aws(A_WV, A_WO)])
                op.then_inc(v_done, 1)

            def scores(b, par, i):
                n = STEPS * b + i
                if i == 0:
                    pe.wait_ge(q_loaded, 16 * (b + 1))
                    pe.wait_ge(k_loaded, 16 * (b + 1))
                if some(2 * n):
                    pe.wait_ge(max_done, 2 * n)
                t, g, o = head_of(i) // 8, head_of(i) % 8 // 2, head_of(i) % 2
                rows, cols = slice(64 * o, 64 * o + 64), slice(S * t, S * t + S)
                q, k = q_stack[rows, par, g, cols], k_stack[rows, par, g, cols]
                product(sc_ps[:, 0:P], [(q[:, 0:P], k[:, 0:P])])
                product(sc_ps[:, P:3 * P], [(q[:, P:S], k[:, 0:S])]).then_inc(scores_done, 1)

            def gate_up(b, par, i, first):
                n = STEPS * b + i
                if i == 0:
                    pe.wait_ge(x_split, b + 1)
                if first:
                    pe.wait_ge(w_ready, i // 2 + 1)
                if some(n - 1):
                    pe.wait_ge(inter_done, n - 1)
                cols = slice(P * (i % 2), P * (i % 2) + P)
                for m in (GATE, UPW):
                    op = product(gu[i % 2][:, S * m:S * m + S],
                                 [p for t in range(KT) for p in
                                  pieces((w_hi[:, i // 2, t, m, cols], w_lo[:, i // 2, t, m, cols]), xT(par, t))])
                op.then_inc(gu_done, 1)

            def transpose_probs(n, i):
                pe.wait_ge(normed, n + 1)
                if some(n):
                    pe.wait_ge(pT_stored, n)
                for c in range(3):
                    op = nc.tensor.transpose(pT_ps[:, P * c:P * c + P], probs[:, i % 2, P * c:P * c + P], ident[:, :])
                op.then_inc(pT_done, 1)

            def down(b, i):
                n = STEPS * b + i
                if i == 0:
                    if some(b):
                        pe.wait_ge(ffn_done, b)
                pe.wait_ge(i_split, n + 1)
                w = w_hi[:, i // 2, i % 2, DOWNW, :], w_lo[:, i // 2, i % 2, DOWNW, :]
                for tt in range(TT):
                    hidden = i_hi[:, i % 4, P * tt:P * tt + P], i_lo[:, i % 4, P * tt:P * tt + P]
                    op = product(acc[:, D * tt:D * tt + D], pieces(hidden, w), begin=i == 0 and tt == 0,
                                 end=i == STEPS - 1, loose=True)
                op.then_inc(down_done, 1)

            def attend(b, par, g):
                pe.wait_ge(pT_stored, STEPS * b + 4 * g + 4)
                if g == 0:
                    pe.wait_ge(v_stored, 4 * (b + 1))
                    if some(b):
                        pe.wait_ge(o_split, b)
                tile, odd = divmod(g, 2)
                for kt, (c0, c1, first_token) in enumerate(((0, S, 0), (S, 3 * P, P))):
                    for quadrant in range(4):
                        i = 4 * g + quadrant
                        r = 32 * quadrant
                        op = nc.tensor.matmul(o_ps[r:r + 32, S * tile + first_token:S * tile + S],
                                              v_pad[:, par, kt, head_of(i), :], pT[:, i % 8, c0:c1],
                                              start=odd == 0 and kt == 0, stop=odd == 1 and kt == 1, skip_group_check=True)
                op.then_inc(pv_done, 1)

            def project(b, batches):
                pe.wait_ge(o_split, b + 1)
                pe.wait_ge(v_stored, 4 * batches)
                for tt in range(TT):
                    tokens = slice(P * tt, P * tt + P)
                    op = product(m1[:, D * tt:D * tt + D],
                                 [p for t in range(2) for p in
                                  pieces((o_hi[:, t, tokens], o_lo[:, t, tokens]), aws(A_WO + D * t, A_WO + D * t + D))])
                op.then_inc(wo_done, 1)

            def batch(b, par, first, last):
                for i in range(STEPS):
                    n = STEPS * b + i
                    scores(b, par, i)
                    gate_up(b, par, i, first)
                    if i >= 2:
                        down(b, i - 2)
                    elif not first:
                        down(b - 1, STEPS - 2 + i)
                    if not (first and i == 0):
                        transpose_probs(n - 1, (i - 1) % STEPS)
                    if i == 1 and not first:
                        attend(b - 1, 1 - par, GROUPS - 1)
                    if i in (5, 9, 13):
                        attend(b, par, i // 4 - 1)
                    if i == 4 and not first:
                        project(b - 1, b + 1)
                    if not last:
                        if i == 3:
                            transpose_tokens(b + 1)
                        if i == 6:
                            latent(b + 1, 1 - par)
                        if i in (7, 8):
                            queries(b + 1, 1 - par, i - 7)
                        if i == 10:
                            keys(b + 1)
                        if i == 11:
                            values(b + 1)

            pe.wait_ge(const_ready, 5)
            transpose_tokens(0)
            pe.wait_ge(aw_ready, 1)
            latent(0, 0)
            queries(0, 0, 0)
            queries(0, 0, 1)
            pe.wait_ge(aw_ready, 2)
            keys(0)
            values(0)
            batch(0, 0, True, False)
            with pe.Fori(0, (B - 2) // 2) as it:
                batch(2 * it + 1, 1, False, False)
                batch(2 * it + 2, 0, False, False)
            batch(B - 1, 1, False, True)
            transpose_probs(STEPS * B - 1, STEPS - 1)
            down(B - 1, STEPS - 2)
            attend(B - 1, 1, GROUPS - 1)
            down(B - 1, STEPS - 1)
            project(B - 1, B)


def kernel(**inputs):
    import numpy as _np
    import concourse.bacc as _bacc
    from concourse.bass_utils import run_bass_kernel_spmd as _run

    a = {k.removeprefix("L0_"): _np.asarray(v) for k, v in inputs.items()}
    def by_byte(w):
        return w.reshape(CHUNKS, P, 2, -1).transpose(3, 0, 2, 1).reshape(-1, CHUNKS, 2 * P)

    def by_unit(w):
        return w.T.reshape(CHUNKS, -1, D).transpose(1, 0, 2)

    packed = _np.stack([by_byte(a["ffn_gate_W_packed"]), by_byte(a["ffn_up_W_packed"]), by_unit(a["ffn_down_W_packed"])], axis=2)
    scales = _np.stack([by_byte(a["ffn_gate_scales"]), by_byte(a["ffn_up_scales"]), by_unit(a["ffn_down_scales"])], axis=2)
    arrays = {
        "x": a["attn_x"], "wq": a["attn_Wq"], "wkv": a["attn_Wkv"], "wk": a["attn_Wk"], "wv": a["attn_Wv"], "wo": a["attn_Wo"],
        "packed": packed.reshape(P, CHUNKS, 3 * S), "scales": scales.reshape(P // 16, CHUNKS, 3 * S),
    }
    arrays = {k: _np.ascontiguousarray(v) for k, v in arrays.items()}
    nc = _bacc.Bacc("TRN2", target_bir_lowering=False, num_devices=1)
    aps = [nc.dram_tensor(k, v.shape, mybir.dt.from_np(v.dtype), kind="ExternalInput").ap() for k, v in arrays.items()]
    out = nc.dram_tensor("out", (B, S, D), F32, kind="ExternalOutput").ap()
    layer(nc, *aps, out)
    return _run(nc, [arrays], core_ids=[0]).results[0]["out"]
```

```python
import numpy as np

import concourse.bass as bass
import concourse.mybir as mybir
from concourse.alu_op_type import AluOpType as ALU
from contextlib import ExitStack

ACT = mybir.ActivationFunctionType
F32, F16, U16, I32 = mybir.dt.float32, mybir.dt.float16, mybir.dt.uint16, mybir.dt.int32

P = 128
B, S, D = 16, 256, 256
H, HD = 16, 16
L = 64
WINDOW, PERSIST = 128, 16
MLP, BLOCK = 2048, 32
TT = S // P
KT = D // P
STEPS = 16
CHUNKS = MLP // (2 * P)
IN_FLIGHT = 4
GROUPS = 4
EPS = 1e-5
UP = 256.0
DOWN = 1.0 / UP
MLP_UP = 64.0
MLP_DOWN = 1.0 / MLP_UP
MASKED = -1e30
GELU_CUBE = 0.044715
GELU_SLOPE = 0.7978845608028654
GATE, UPW, DOWNW = range(3)


def head_of(step):
    group, quadrant = divmod(step, 4)
    return 8 * (group // 2) + 2 * quadrant + group % 2


def some(count):
    return not isinstance(count, int) or count > 0


def layer(nc, x, wq, wkv, wk, wv, wo, packed, scales, out):
    ctx = ExitStack()
    with ctx:
        def sb(name, shape, dtype=F32):
            return ctx.enter_context(nc.sbuf_tensor(name, shape, dtype))

        def bank(name):
            return ctx.enter_context(nc.psum_tensor(name, [P, 512], F32))

        def sem(name):
            return ctx.enter_context(nc.semaphore(name))

        ident = sb("ident", [P, P])
        mask = sb("mask", [P, 3 * P])
        x_in = sb("x_in", [P, TT, D])
        x_res = sb("x_res", [P, TT, D])
        bn = sb("bn", [P, TT, 6])
        mv = sb("mv", [P, TT, 2])
        nm = sb("nm", [P, TT])
        ve = sb("ve", [P, TT])
        minus_half = sb("minus_half", [P, TT])
        rstd = sb("rstd", [P, TT])
        xn = sb("xn", [P, TT, D])
        xT_hi = sb("xT_hi", [P, 2, KT, S], F16)
        xT_lo = sb("xT_lo", [P, 2, KT, S], F16)
        A_WQ, A_WKV, A_WK, A_WV, A_WO, A_END = 0, 512, 768, 1024, 1280, 1792
        aw = sb("aw", [P, A_END])
        aw_hi = sb("aw_hi", [P, A_END], F16)
        aw_lo = sb("aw_lo", [P, A_END], F16)
        lat = sb("lat", [P, S], F16)
        q_pieces = sb("q_pieces", [P, 2, 2, S], F16)
        k_pieces = sb("k_pieces", [P, 2, 2, S], F16)
        q_stack = sb("q_stack", [P, 2, H // 4, 2 * S], F16)
        k_stack = sb("k_stack", [P, 2, H // 4, 2 * S], F16)
        v_pad = sb("v_pad", [P, 2, TT, H, 2 * HD])
        s_neg = sb("s_neg", [P, 2, 3 * P])
        nmax = sb("nmax", [P, 2, TT])
        probs = sb("probs", [P, 2, 3 * P])
        rowsum = sb("rowsum", [P, 2, TT])
        rrow = sb("rrow", [P, 2, TT])
        pT = sb("pT", [P, 8, 3 * P])
        o_hi = sb("o_hi", [P, 2, S], F16)
        o_lo = sb("o_lo", [P, 2, S], F16)
        sq = sb("sq", [P, 2, S])
        poly = sb("poly", [P, 2, S])
        th = sb("th", [P, 2, S])
        gelu = sb("gelu", [P, 2, S])
        inter = sb("inter", [P, 2, S])
        i_hi = sb("i_hi", [P, 4, S], F16)
        i_lo = sb("i_lo", [P, 4, S], F16)
        ffn = sb("ffn", [P, TT * D])
        o_sb = sb("o_sb", [P, TT * D])
        pk = sb("pk", [P, IN_FLIGHT, 3 * S], I32)
        sc = sb("sc", [P, IN_FLIGHT, 3 * S])
        code = sb("code", [P, 2, 3 * S], U16)
        sign = sb("sign", [P, 2, 2, 3 * S], U16)
        low = sb("low", [P, 2, 3 * S], F16)
        wf = sb("wf", [P, 2, 2, 3 * S])
        w_hi = sb("w_hi", [P, CHUNKS, 2, 3, S], F16)
        w_lo = sb("w_lo", [P, CHUNKS, 2, 3, S], F16)
        q_dram = nc.dram_tensor("q_rows", [2, P, 4, 2 * S], F16, kind="Internal").ap()
        k_dram = nc.dram_tensor("k_rows", [2, P, 4, 2 * S], F16, kind="Internal").ap()

        gu = [bank("gu0"), bank("gu1")]
        acc = bank("acc")
        sc_ps = bank("sc_ps")
        pT_ps = bank("pT_ps")
        o_ps = bank("o_ps")
        m0 = bank("m0")
        m1 = bank("m1")

        aw_loaded, aw_hi_done, aw_ready = [sem(f"aw_loaded{lot}") for lot in range(3)], sem("aw_hi_done"), sem("aw_ready")
        pk_loaded = [sem(f"pk_loaded{c}") for c in range(CHUNKS)]
        decode = sem("decode")
        w_float = [sem(f"w_float{c}") for c in range(CHUNKS)]
        w_signed, w_hi_done, w_ready = sem("w_signed"), sem("w_hi_done"), sem("w_ready")
        const_step, const_ready = sem("const_step"), sem("const_ready")
        passed = sem("passed")
        x_loaded, res_loaded = sem("x_loaded"), sem("res_loaded")
        bn_done, aggr_done, stats_ready = sem("bn_done"), sem("aggr_done"), sem("stats_ready")
        rstd_done, xn_ready = sem("rstd_done"), sem("xn_ready")
        x_transposed, x_hi_done, x_split = sem("x_transposed"), sem("x_hi_done"), sem("x_split")
        lat_done, lat_hi_done, lat_split = sem("lat_done"), sem("lat_hi_done"), sem("lat_split")
        q_done, q_hi_done, q_split = sem("q_done"), sem("q_hi_done"), sem("q_split")
        k_done, k_hi_done, k_split = sem("k_done"), sem("k_hi_done"), sem("k_split")
        v_done, v_stored = sem("v_done"), sem("v_stored")
        q_rows_stored, k_rows_stored = sem("q_rows_stored"), sem("k_rows_stored")
        q_loaded, k_loaded, rest_loaded = sem("q_loaded"), sem("k_loaded"), sem("rest_loaded")
        scores_done, max_done, exp_done = sem("scores_done"), sem("max_done"), sem("exp_done")
        recip_done, normed = sem("recip_done"), sem("normed")
        pT_done, pT_stored, pv_done = sem("pT_done"), sem("pT_stored"), sem("pv_done")
        o_hi_done, o_split, wo_done = sem("o_hi_done"), sem("o_split"), sem("wo_done")
        gu_done, sq_done, poly_done = sem("gu_done"), sem("sq_done"), sem("poly_done")
        th_done, gelu_done, inter_done = sem("th_done"), sem("gelu_done"), sem("inter_done")
        i_hi_done, i_split, down_done = sem("i_hi_done"), sem("i_split"), sem("down_done")
        ffn_done, out_ready, out_stored = sem("ffn_done"), sem("out_ready"), sem("out_stored")

        def alone(eng):
            eng.sem_inc(passed, 1)

        x_tok = x.rearrange("b (t p) d -> b p t d", p=P)
        out_tok = out.rearrange("b (t p) d -> b p t d", p=P)
        Q_STORES, K_STORES = 1, 2

        block = ctx.enter_context(nc.Block())

        @block.sync
        def _(sp):
            def load_tokens(b):
                sp.dma_start(x_in[:, :, :], x_tok[b]).then_inc(x_loaded, 16)

            def store_rows(b, par):
                sp.wait_ge(q_split, b + 1)
                sp.dma_start(q_dram[par].rearrange("p (twice c) n -> p twice (c n)", twice=2),
                             q_pieces[:, :].rearrange("p (one c) t s -> p one (c t s)", one=1).to_broadcast([P, 2, 4 * S])).then_inc(q_rows_stored, 16)
                sp.wait_ge(k_split, b + 1)
                for first_row in range(2):
                    sp.dma_start(k_dram[par, :, first_row:4:2], k_pieces[:, :].rearrange("p c t s -> p c (t s)")).then_inc(k_rows_stored, 16)

            def stack_rows(dram, par):
                return dram[par].rearrange("(g o d) c n -> o (d c) g n", o=2, d=HD)

            def load_stacks(b, par):
                sp.wait_ge(q_rows_stored, 16 * Q_STORES * (b + 1))
                sp.dma_start(q_stack[:, par, :, :], q_dram[par].rearrange("(g o d) c n -> (o d c) g n", o=2, d=HD)).then_inc(q_loaded, 16)
                sp.wait_ge(k_rows_stored, 16 * K_STORES * (b + 1))
                sp.dma_start(k_stack[:, par, :, :], k_dram[par].rearrange("(g o d) c n -> (o d c) g n", o=2, d=HD)).then_inc(k_loaded, 16)

            def batch(b, par, first, last):
                if not (first or last):
                    sp.wait_ge(xn_ready, TT * (b + 1))
                    alone(sp)
                    load_tokens(b + 1)
                if some(b):
                    sp.wait_ge(ffn_done, b)
                alone(sp)
                sp.dma_start(x_res[:, :, :], x_tok[b]).then_inc(res_loaded, 16)
                if not first:
                    if some(b):
                        sp.wait_ge(out_ready, b)
                    alone(sp)
                    sp.dma_start(out_tok[b - 1], o_sb[:, :].rearrange("p (t d) -> p t d", t=TT)).then_inc(out_stored, 16)
                if not last:
                    store_rows(b + 1, 1 - par)
                    if some(STEPS * b):
                        sp.wait_ge(scores_done, STEPS * b)
                    alone(sp)
                    load_stacks(b + 1, 1 - par)

            load_tokens(0)
            sp.dma_start(aw[:, A_WKV:A_WK].rearrange("p (t c n) -> p t c n", t=KT, c=2),
                         wkv.rearrange("(p t c) n -> p t c n", t=KT, c=1).to_broadcast([P, KT, 2, L])).then_inc(aw_loaded[0], 16)
            sp.dma_start(aw[:, A_WQ:A_WKV].rearrange("p (t n) -> p t n", t=KT),
                         wq.rearrange("(p t) n -> p t n", t=KT)).then_inc(aw_loaded[0], 16)

            def load_chunk(c):
                if c >= IN_FLIGHT:
                    sp.wait_ge(w_float[c - IN_FLIGHT], 1)
                sp.dma_start(pk[:, c % IN_FLIGHT, :], packed[:, c, :]).then_inc(pk_loaded[c], 16)
                sp.dma_start(sc[:, c % IN_FLIGHT, :],
                             scales[:, c:c + 1, :].to_broadcast([P // 16, 16, 3 * S])).then_inc(pk_loaded[c], 16)

            load_chunk(0)
            for c0, w in ((A_WK, wk), (A_WV, wv)):
                sp.dma_start(aw[:, c0:c0 + D], w.rearrange("(c l) n -> c l n", c=1).to_broadcast([2, L, D])).then_inc(aw_loaded[1], 16)
            load_chunk(1)
            load_chunk(2)
            store_rows(0, 0)
            for rows, q_sem, k_sem in ((slice(0, P // 2), q_loaded, k_loaded), (slice(P // 2, P), rest_loaded, rest_loaded)):
                half = rows.start // (P // 2)
                sp.wait_ge(q_rows_stored, 16 * Q_STORES)
                sp.dma_start(q_stack[rows, 0, :, :], stack_rows(q_dram, 0)[half]).then_inc(q_sem, 16)
                sp.wait_ge(k_rows_stored, 16 * K_STORES)
                sp.dma_start(k_stack[rows, 0, :, :], stack_rows(k_dram, 0)[half]).then_inc(k_sem, 16)
            sp.wait_ge(xn_ready, TT)
            load_tokens(1)
            sp.dma_start(aw[:, A_WO:A_END].rearrange("p (t n) -> p t n", t=2),
                         wo.rearrange("(t p) n -> p t n", t=2)).then_inc(aw_loaded[2], 16)
            for c in range(3, CHUNKS):
                load_chunk(c)
            batch(0, 0, True, False)
            with sp.Fori(0, (B - 2) // 2) as it:
                batch(2 * it + 1, 1, False, False)
                batch(2 * it + 2, 0, False, False)
            batch(B - 1, 1, False, True)
            sp.wait_ge(out_ready, B)
            sp.dma_start(out_tok[B - 1], o_sb[:, :].rearrange("p (t d) -> p t d", t=TT)).then_inc(out_stored, 16)
            sp.wait_ge(out_stored, 16 * B)

        @block.gpsimd
        def _(pool):
            def scaled(c):
                if c >= 2:
                    pool.wait_ge(w_ready, c - 1)
                pool.wait_ge(w_signed, c + 1)
                nc.gpsimd.tensor_tensor(wf[:, c % 2], sign[:, c % 2].bitcast(F16),
                                        sc[:, c % IN_FLIGHT:c % IN_FLIGHT + 1, :].to_broadcast([P, 2, 3 * S]),
                                        ALU.mult).then_inc(w_float[c], 1)

            def weights_lo(c):
                pool.wait_ge(w_hi_done, c + 1)
                nc.gpsimd.tensor_tensor(w_lo[:, c].rearrange("p a m n -> p (a m n)"),
                                        wf[:, c % 2].rearrange("p a n -> p (a n)"),
                                        w_hi[:, c].rearrange("p a m n -> p (a m n)"), ALU.subtract).then_inc(w_ready, 1)

            def inverse_deviation(b):
                pool.wait_ge(stats_ready, 2 * (b + 1))
                nc.gpsimd.tensor_tensor(rstd[:, :], ve[:, :], minus_half[:, :], ALU.pow).then_inc(rstd_done, 1)

            def norm_tokens(b, t):
                pool.wait_ge(rstd_done, b + 1)
                if some(b):
                    pool.wait_ge(x_transposed, b)
                alone(pool)
                nc.gpsimd.tensor_scalar(xn[:, t, :], x_in[:, t, :], nm[:, t:t + 1], rstd[:, t:t + 1],
                                        ALU.add, ALU.mult).then_inc(xn_ready, 1)

            def intermediate_lo(n, i):
                pool.wait_ge(i_hi_done, n + 1)
                nc.gpsimd.tensor_tensor(i_lo[:, i % 4, :], inter[:, i % 2, :], i_hi[:, i % 4, :],
                                        ALU.subtract).then_inc(i_split, 1)

            def scale_probs(n, i):
                pool.wait_ge(recip_done, n + 1)
                alone(pool)
                r = i % 2
                nc.gpsimd.tensor_scalar(probs[:, r, 0:P], probs[:, r, 0:P], rrow[:, r, 0:1], 1.0, ALU.mult, ALU.mult)
                nc.gpsimd.tensor_scalar(probs[:, r, P:3 * P], probs[:, r, P:3 * P], rrow[:, r, 1:2], 1.0,
                                        ALU.mult, ALU.mult).then_inc(normed, 1)

            def batch(b, par, first, last):
                for i in range(STEPS):
                    n = STEPS * b + i
                    if not (first and i == 0):
                        intermediate_lo(n - 1, (i - 1) % STEPS)
                    if not first:
                        scale_probs(n, i)
                    if first and i % 2 == 1 and i // 2 + 3 < CHUNKS:
                        scaled(i // 2 + 3)
                    if i == 1 and not last:
                        inverse_deviation(b + 1)
                        norm_tokens(b + 1, 0)
                    if i == 2 and not last:
                        norm_tokens(b + 1, 1)
                    if first and i % 2 == 0 and i > 0 and i // 2 + 1 < CHUNKS:
                        weights_lo(i // 2 + 1)

            nc.gpsimd.memset(ident[:, :], 0.0).then_inc(const_step, 1)
            nc.gpsimd.memset(mask[:, :], 0.0).then_inc(const_step, 1)
            nc.gpsimd.memset(minus_half[:, :], -0.5).then_inc(const_step, 1)
            nc.gpsimd.memset(v_pad[:, :, :, :, :], 0.0).then_inc(const_ready, 1)
            pool.wait_ge(const_step, 3)
            nc.gpsimd.affine_select(out=ident[:, :], in_=ident[:, :], compare_op=ALU.not_equal, fill=1.0, base=0,
                                    pattern=[[-1, P]], channel_multiplier=1).then_inc(const_ready, 1)
            for c0 in (0, 2 * P):
                nc.gpsimd.affine_select(out=mask[:, c0:c0 + P], in_=mask[:, c0:c0 + P], compare_op=ALU.is_ge,
                                        fill=MASKED, base=0, pattern=[[-1, P]], channel_multiplier=1).then_inc(const_ready, 1)
            nc.gpsimd.affine_select(out=mask[:, P + PERSIST:2 * P], in_=mask[:, P + PERSIST:2 * P], compare_op=ALU.is_ge,
                                    fill=MASKED, base=PERSIST - (P - WINDOW) - 1, pattern=[[1, P - PERSIST]],
                                    channel_multiplier=-1).then_inc(const_ready, 1)
            inverse_deviation(0)
            norm_tokens(0, 0)
            norm_tokens(0, 1)
            weights_lo(0)
            scaled(1)
            weights_lo(1)
            scaled(2)
            batch(0, 0, True, False)
            with pool.Fori(0, (B - 2) // 2) as it:
                batch(2 * it + 1, 1, False, False)
                batch(2 * it + 2, 0, False, False)
            batch(B - 1, 1, False, True)
            intermediate_lo(STEPS * B - 1, STEPS - 1)

        @block.scalar
        def _(act):
            def hi_piece(dst, src, scale, done):
                nc.scalar.activation(dst, src, ACT.Copy, scale=scale).then_inc(done, 1)

            def weights_hi(c):
                act.wait_ge(w_float[c], 1)
                hi_piece(w_hi[:, c].rearrange("p a m n -> p (a m n)"), wf[:, c % 2].rearrange("p a n -> p (a n)"), 1.0, w_hi_done)

            def weights_of_attention(part, loads, c0, c1):
                act.wait_ge(aw_loaded[part], 16 * loads)
                hi_piece(aw_hi[:, c0:c1], aw[:, c0:c1], UP, aw_hi_done)

            def tokens_hi(b, par):
                act.wait_ge(x_transposed, b + 1)
                hi_piece(xT_hi[:, par], m0[:, :].rearrange("p (t s) -> p t s", t=KT), 1.0, x_hi_done)

            def latent_hi(b):
                if some(b):
                    act.wait_ge(v_done, b)
                act.wait_ge(lat_done, b + 1)
                hi_piece(lat[:, :], m0[:, 0:S], DOWN, lat_hi_done)

            def queries_hi(b):
                if some(b):
                    act.wait_ge(q_rows_stored, 16 * Q_STORES * b)
                act.wait_ge(q_done, b + 1)
                hi_piece(q_pieces[:, 0], m1[:, :].rearrange("p (t s) -> p t s", t=2), DOWN, q_hi_done)

            def keys_hi(b):
                if some(b):
                    act.wait_ge(k_rows_stored, 16 * K_STORES * b)
                act.wait_ge(k_done, b + 1)
                hi_piece(k_pieces[:, 0], m0[:, :].rearrange("p (t s) -> p t s", t=2), DOWN, k_hi_done)

            def values_store(b, par, t):
                act.wait_ge(v_done, b + 1)
                if some(GROUPS * (b - 1)):
                    act.wait_ge(pv_done, GROUPS * (b - 1))
                for odd in range(2):
                    dst = v_pad[:, par, t, odd:H:2, HD * odd:HD * odd + HD]
                    src = m1[:, D * t:D * t + D].rearrange("p (h d) -> p h d", d=HD)[:, odd:H:2, :]
                    hi_piece(dst, src, DOWN, v_stored)

            def attention_hi(b):
                if some(b):
                    act.wait_ge(wo_done, b)
                act.wait_ge(pv_done, GROUPS * (b + 1))
                hi_piece(o_hi[:, :, :], o_ps[:, :].rearrange("p (t s) -> p t s", t=2), 1.0, o_hi_done)

            def exponentials(n, i):
                if some(n - 1):
                    act.wait_ge(pT_done, n - 1)
                act.wait_ge(max_done, 2 * (n + 1))
                r = i % 2
                nc.scalar.activation(probs[:, r, 0:P], s_neg[:, r, 0:P], ACT.Exp, bias=nmax[:, r, 0:1], scale=-1.0,
                                     accum_out=rowsum[:, r, 0:1])
                nc.scalar.activation(probs[:, r, P:3 * P], s_neg[:, r, P:3 * P], ACT.Exp, bias=nmax[:, r, 1:2], scale=-1.0,
                                     accum_out=rowsum[:, r, 1:2]).then_inc(exp_done, 1)

            def scale_probs(n, i):
                act.wait_ge(recip_done, n + 1)
                r = i % 2
                nc.scalar.activation(probs[:, r, 0:P], probs[:, r, 0:P], ACT.Copy, scale=rrow[:, r, 0:1])
                nc.scalar.activation(probs[:, r, P:3 * P], probs[:, r, P:3 * P], ACT.Copy,
                                     scale=rrow[:, r, 1:2]).then_inc(normed, 1)

            def squares(n, i):
                act.wait_ge(gu_done, n + 1)
                nc.scalar.activation(sq[:, i % 2, :], gu[i % 2][:, 0:S], ACT.Square,
                                     scale=GELU_CUBE ** 0.5 * MLP_DOWN).then_inc(sq_done, 1)

            def tanhs(n, i):
                act.wait_ge(poly_done, n + 1)
                nc.scalar.activation(th[:, i % 2, :], poly[:, i % 2, :], ACT.Tanh, scale=GELU_SLOPE * MLP_DOWN).then_inc(th_done, 1)

            def store_pT(b, i):
                n = STEPS * b + i
                if i % 4 == 0:
                    if some(GROUPS * b + i // 4 - 1):
                        act.wait_ge(pv_done, GROUPS * b + i // 4 - 1)
                act.wait_ge(pT_done, n + 1)
                nc.scalar.activation(pT[:, i % 8, :], pT_ps[:, 0:3 * P], ACT.Copy).then_inc(pT_stored, 1)

            def batch(b, par, first, last):
                for i in range(STEPS):
                    n = STEPS * b + i
                    exponentials(n, i)
                    squares(n, i)
                    if not (first and i == 0):
                        if i == 0:
                            store_pT(b - 1, STEPS - 1)
                        else:
                            store_pT(b, i - 1)
                    if i == 2 and not first:
                        attention_hi(b - 1)
                    if not last:
                        if i == 3:
                            tokens_hi(b + 1, 1 - par)
                        if i == 6:
                            latent_hi(b + 1)
                        if i == 8:
                            queries_hi(b + 1)
                        if i == 10:
                            keys_hi(b + 1)
                        if i in (11, 12):
                            values_store(b + 1, 1 - par, i - 11)
                    if first:
                        scale_probs(n, i)
                    tanhs(n, i)
                    if first and i % 2 == 1 and i // 2 + 2 < CHUNKS:
                        weights_hi(i // 2 + 2)
                    if first and i == STEPS - 3:
                        weights_of_attention(2, 1, A_WO, A_END)

            weights_of_attention(0, 2, 0, A_WK)
            act.wait_ge(const_ready, 5)
            tokens_hi(0, 0)
            weights_of_attention(1, 2, A_WK, A_WO)
            latent_hi(0)
            queries_hi(0)
            keys_hi(0)
            weights_hi(0)
            values_store(0, 0, 0)
            values_store(0, 0, 1)
            weights_hi(1)
            batch(0, 0, True, False)
            with act.Fori(0, (B - 2) // 2) as it:
                batch(2 * it + 1, 1, False, False)
                batch(2 * it + 2, 0, False, False)
            batch(B - 1, 1, False, True)
            store_pT(B - 1, STEPS - 1)
            attention_hi(B - 1)

        @block.vector
        def _(dve):
            code_all = code[:, :, :].rearrange("p a n -> p (a n)")
            low_all = low[:, :, :].rearrange("p a n -> p (a n)")
            DECODE_STEPS = 5

            def sign_all(c):
                return sign[:, c % 2].rearrange("p a n -> p (a n)")

            def extract(c):
                dve.wait_ge(pk_loaded[c], 16 * 2)
                byte = pk[:, c % IN_FLIGHT, :].bitcast(U16).rearrange("p (n two) -> p n two", two=2)[:, :, 0]
                for nibble, shift in ((0, 9), (1, 5)):
                    op = nc.vector.tensor_scalar(code[:, nibble, :], byte, shift, 0x1E00, ALU.logical_shift_left, ALU.bitwise_and)
                op.then_inc(decode, 1)

            def signs(c):
                if c >= 2:
                    dve.wait_ge(w_float[c - 2], 1)
                dve.wait_ge(decode, DECODE_STEPS * c + 1)
                nc.vector.tensor_scalar(sign_all(c), code_all, 0x1000, 3, ALU.bitwise_and, ALU.logical_shift_left).then_inc(decode, 1)

            def magnitudes(c):
                dve.wait_ge(decode, DECODE_STEPS * c + 2)
                nc.vector.tensor_scalar(code_all, code_all, 0x0E00, 0x5000, ALU.bitwise_and, ALU.bitwise_or).then_inc(decode, 1)

            def corrections(c):
                dve.wait_ge(decode, DECODE_STEPS * c + 3)
                nc.vector.tensor_scalar(low_all, code_all.bitcast(F16), -64.0, 0.0, ALU.add, ALU.min).then_inc(decode, 1)

            def corrected(c):
                dve.wait_ge(decode, DECODE_STEPS * c + 4)
                nc.vector.tensor_tensor(low_all, low_all, code_all.bitcast(F16), ALU.add).then_inc(decode, 1)

            def signed(c):
                dve.wait_ge(decode, DECODE_STEPS * c + 5)
                nc.vector.tensor_tensor(sign_all(c), sign_all(c), low_all.bitcast(U16), ALU.bitwise_xor).then_inc(w_signed, 1)

            def scaled(c):
                if some(c - 1):
                    dve.wait_ge(w_ready, c - 1)
                dve.wait_ge(w_signed, c + 1)
                nc.vector.scalar_tensor_tensor(out=wf[:, c % 2], in0=sign[:, c % 2].bitcast(F16), scalar=1.0,
                                               in1=sc[:, c % IN_FLIGHT:c % IN_FLIGHT + 1, :].to_broadcast([P, 2, 3 * S]),
                                               op0=ALU.mult, op1=ALU.mult).then_inc(w_float[c], 1)

            def lo_piece(dst, src, hi, scale, done):
                nc.vector.scalar_tensor_tensor(out=dst, in0=src, scalar=scale, in1=hi,
                                               op0=ALU.mult, op1=ALU.subtract).then_inc(done, 1)

            def weights_of_attention(part, c0, c1):
                dve.wait_ge(aw_hi_done, part + 1)
                lo_piece(aw_lo[:, c0:c1], aw[:, c0:c1], aw_hi[:, c0:c1], UP, aw_ready)

            def stats(b):
                dve.wait_ge(x_loaded, 16 * (b + 1))
                for t in range(TT):
                    op = nc.vector.bn_stats(bn[:, t, :], x_in[:, t, :])
                op.then_inc(bn_done, 1)

            def moments(b):
                dve.wait_ge(bn_done, b + 1)
                alone(dve)
                for t in range(TT):
                    op = nc.vector.bn_aggr(mv[:, t, :], bn[:, t, :])
                op.then_inc(aggr_done, 1)
                dve.wait_ge(aggr_done, b + 1)
                nc.vector.tensor_scalar(nm[:, :], mv[:, :, 0], -1.0, None, ALU.mult).then_inc(stats_ready, 1)
                nc.vector.tensor_scalar(ve[:, :], mv[:, :, 1], EPS, None, ALU.add).then_inc(stats_ready, 1)

            def tokens_lo(b, par):
                dve.wait_ge(x_hi_done, b + 1)
                lo_piece(xT_lo[:, par], m0[:, :].rearrange("p (t s) -> p t s", t=KT), xT_hi[:, par], 1.0, x_split)

            def latent_lo(b):
                dve.wait_ge(lat_hi_done, b + 1)
                lo_piece(lat[L:P, :], m0[L:P, 0:S], lat[L:P, :], DOWN, lat_split)

            def queries_lo(b):
                dve.wait_ge(q_hi_done, b + 1)
                lo_piece(q_pieces[:, 1], m1[:, :].rearrange("p (t s) -> p t s", t=2), q_pieces[:, 0], DOWN, q_split)

            def keys_lo(b):
                dve.wait_ge(k_hi_done, b + 1)
                lo_piece(k_pieces[:, 1], m0[:, :].rearrange("p (t s) -> p t s", t=2), k_pieces[:, 0], DOWN, k_split)

            def attention_lo(b):
                dve.wait_ge(o_hi_done, b + 1)
                lo_piece(o_lo[:, :, :], o_ps[:, :].rearrange("p (t s) -> p t s", t=2), o_hi[:, :, :], 1.0, o_split)

            def add_ffn(b):
                dve.wait_ge(down_done, STEPS * (b + 1))
                dve.wait_ge(res_loaded, 16 * (b + 1))
                nc.vector.scalar_tensor_tensor(out=ffn[:, :], in0=acc[:, :], scalar=MLP_DOWN,
                                               in1=x_res[:, :, :].rearrange("p t d -> p (t d)"),
                                               op0=ALU.mult, op1=ALU.add).then_inc(ffn_done, 1)

            def add_attention(b):
                if some(16 * b):
                    dve.wait_ge(out_stored, 16 * b)
                dve.wait_ge(wo_done, b + 1)
                dve.wait_ge(ffn_done, b + 1)
                nc.vector.scalar_tensor_tensor(out=o_sb[:, :], in0=m1[:, :], scalar=DOWN, in1=ffn[:, :],
                                               op0=ALU.mult, op1=ALU.add).then_inc(out_ready, 1)

            def maxima(n, i):
                if some(n - 1):
                    dve.wait_ge(exp_done, n - 1)
                dve.wait_ge(scores_done, n + 1)
                alone(dve)
                r = i % 2
                for t, (c0, c1) in enumerate(((0, P), (P, 3 * P))):
                    nc.vector.tensor_tensor_reduce(out=s_neg[:, r, c0:c1], in0=sc_ps[:, c0:c1], in1=mask[:, c0:c1],
                                                   scale=-1.0 / HD ** 0.5, scalar=3e38, op0=ALU.add, op1=ALU.min,
                                                   accum_out=nmax[:, r, t:t + 1]).then_inc(max_done, 1)

            def reciprocals(n, i):
                dve.wait_ge(exp_done, n + 1)
                nc.vector.reciprocal(rrow[:, i % 2, :], rowsum[:, i % 2, :]).then_inc(recip_done, 1)

            def polynomial(n, i):
                dve.wait_ge(sq_done, n + 1)
                nc.vector.scalar_tensor_tensor(out=poly[:, i % 2, :], in0=sq[:, i % 2, :], scalar=1.0,
                                               in1=gu[i % 2][:, 0:S], op0=ALU.add, op1=ALU.mult).then_inc(poly_done, 1)

            def twice_gelu(n, i):
                dve.wait_ge(th_done, n + 1)
                nc.vector.scalar_tensor_tensor(out=gelu[:, i % 2, :], in0=th[:, i % 2, :], scalar=1.0,
                                               in1=gu[i % 2][:, 0:S], op0=ALU.add, op1=ALU.mult).then_inc(gelu_done, 1)

            def gated(n, i):
                if some(n - 1):
                    dve.wait_ge(i_split, n - 1)
                dve.wait_ge(gelu_done, n + 1)
                nc.vector.scalar_tensor_tensor(out=inter[:, i % 2, :], in0=gelu[:, i % 2, :], scalar=0.5 * MLP_DOWN * MLP_DOWN,
                                               in1=gu[i % 2][:, S:2 * S], op0=ALU.mult, op1=ALU.mult).then_inc(inter_done, 1)

            def intermediate_hi(n, i):
                if some(n - 3):
                    dve.wait_ge(down_done, n - 3)
                dve.wait_ge(inter_done, n + 1)
                nc.vector.tensor_copy(i_hi[:, i % 4, :], inter[:, i % 2, :]).then_inc(i_hi_done, 1)

            def batch(b, par, first, last):
                for i in range(STEPS):
                    n = STEPS * b + i
                    before = (i - 1) % STEPS
                    c = i // 2 + 3
                    begins = first and i % 2 == 0 and i > 0 and c < CHUNKS
                    ends = first and i % 2 == 1 and c < CHUNKS
                    if i == 2 and not first:
                        add_ffn(b - 1)
                    maxima(n, i)
                    if first and i == 0:
                        corrected(2)
                    if first and i == 1:
                        extract(3)
                    if begins:
                        extract(c)
                    if not (first and i == 0):
                        twice_gelu(n - 1, before)
                    if first and i == 1:
                        signs(3)
                        magnitudes(3)
                    if begins:
                        signs(c)
                    if ends and i > 1:
                        corrected(c)
                    if i == 3 and not first:
                        attention_lo(b - 1)
                    if i == 5 and not first:
                        add_attention(b - 1)
                    if not last:
                        if i == 0 and not first:
                            stats(b + 1)
                        if i == 1:
                            moments(b + 1)
                        if i == 4:
                            tokens_lo(b + 1, 1 - par)
                        if i == 7:
                            latent_lo(b + 1)
                        if i == 9:
                            queries_lo(b + 1)
                        if i == 11:
                            keys_lo(b + 1)
                    if not (first and i == 0):
                        gated(n - 1, before)
                    if first and i == 1:
                        corrections(3)
                    reciprocals(n, i)
                    if first and i == 0:
                        signed(2)
                    if first and i == 1:
                        corrected(3)
                    if begins:
                        magnitudes(c)
                    if ends:
                        signed(c)
                    if not (first and i == 0):
                        intermediate_hi(n - 1, before)
                    polynomial(n, i)
                    if first and i == 0:
                        stats(b + 1)
                    if begins:
                        corrections(c)
                    if first and i == STEPS - 2:
                        weights_of_attention(2, A_WO, A_END)

            stats(0)
            moments(0)
            weights_of_attention(0, 0, A_WK)
            extract(0)
            signs(0)
            magnitudes(0)
            dve.wait_ge(const_ready, 5)
            tokens_lo(0, 0)
            weights_of_attention(1, A_WK, A_WO)
            corrections(0)
            corrected(0)
            latent_lo(0)
            signed(0)
            queries_lo(0)
            keys_lo(0)
            scaled(0)
            extract(1)
            signs(1)
            magnitudes(1)
            corrections(1)
            corrected(1)
            signed(1)
            extract(2)
            signs(2)
            magnitudes(2)
            corrections(2)
            batch(0, 0, True, False)
            with dve.Fori(0, (B - 2) // 2) as it:
                batch(2 * it + 1, 1, False, False)
                batch(2 * it + 2, 0, False, False)
            batch(B - 1, 1, False, True)
            end, at = STEPS * B - 1, STEPS - 1
            twice_gelu(end, at)
            gated(end, at)
            intermediate_hi(end, at)
            attention_lo(B - 1)
            add_ffn(B - 1)
            add_attention(B - 1)

        @block.tensor
        def _(pe):
            def product(out_, terms, begin=True, end=True, loose=False):
                for j, (w, m) in enumerate(terms):
                    op = nc.tensor.matmul(out_, w, m, start=begin and j == 0, stop=end and j == len(terms) - 1,
                                          skip_group_check=loose)
                return op

            def pieces(w, m):
                (wh, wl), (mh, ml) = w, m
                return [(wh, mh), (wh, ml), (wl, mh)]

            def xT(par, t):
                return xT_hi[:, par, t, :], xT_lo[:, par, t, :]

            def aws(c0, c1):
                return aw_hi[:, c0:c1], aw_lo[:, c0:c1]

            def transpose_tokens(b):
                pe.wait_ge(xn_ready, TT * (b + 1))
                if some(b):
                    pe.wait_ge(k_split, b)
                for t in range(KT):
                    for tt in range(TT):
                        op = nc.tensor.transpose(m0[:, S * t + P * tt:S * t + P * tt + P], xn[:, tt, t:D:KT], ident[:, :])
                op.then_inc(x_transposed, 1)

            def latent(b, par):
                pe.wait_ge(x_split, b + 1)
                product(m0[:, 0:S], [p for t in range(KT) for p in
                                     pieces(aws(A_WKV + P * t, A_WKV + P * t + P), xT(par, t))]).then_inc(lat_done, 1)

            def queries(b, par, tile):
                if tile == 0:
                    if some(b - 1):
                        pe.wait_ge(out_ready, b - 1)
                op = product(m1[:, S * tile:S * tile + S],
                             [p for t in range(KT) for p in
                              pieces(aws(A_WQ + D * t + P * tile, A_WQ + D * t + P * tile + P), xT(par, t))])
                if tile == 1:
                    op.then_inc(q_done, 1)

            def keys(b):
                pe.wait_ge(lat_split, b + 1)
                for tile in range(2):
                    c0 = A_WK + P * tile
                    op = product(m0[:, S * tile:S * tile + S], [(w, lat[:, :]) for w in aws(c0, c0 + P)])
                op.then_inc(k_done, 1)

            def values(b):
                pe.wait_ge(q_split, b + 1)
                for tt in range(TT):
                    op = product(m1[:, D * tt:D * tt + D], [(lat[:, P * tt:P * tt + P], w) for w in aws(A_WV, A_WO)])
                op.then_inc(v_done, 1)

            def scores(b, par, i, first):
                n = STEPS * b + i
                if i == 0:
                    pe.wait_ge(q_loaded, 16 * (b + 1))
                    pe.wait_ge(k_loaded, 16 * (b + 1))
                if i == 4 and first:
                    pe.wait_ge(rest_loaded, 16 * 2)
                if some(2 * n):
                    pe.wait_ge(max_done, 2 * n)
                t, g, o = head_of(i) // 8, head_of(i) % 8 // 2, head_of(i) % 2
                rows, cols = slice(64 * o, 64 * o + 64), slice(S * t, S * t + S)
                q, k = q_stack[rows, par, g, cols], k_stack[rows, par, g, cols]
                product(sc_ps[:, 0:P], [(q[:, 0:P], k[:, 0:P])])
                product(sc_ps[:, P:3 * P], [(q[:, P:S], k[:, 0:S])]).then_inc(scores_done, 1)

            def gate_up(b, par, i, first):
                n = STEPS * b + i
                if i == 0:
                    pe.wait_ge(x_split, b + 1)
                if first:
                    pe.wait_ge(w_ready, i // 2 + 1)
                if some(n - 1):
                    pe.wait_ge(inter_done, n - 1)
                cols = slice(P * (i % 2), P * (i % 2) + P)
                for m in (GATE, UPW):
                    op = product(gu[i % 2][:, S * m:S * m + S],
                                 [p for t in range(KT) for p in
                                  pieces((w_hi[:, i // 2, t, m, cols], w_lo[:, i // 2, t, m, cols]), xT(par, t))])
                op.then_inc(gu_done, 1)

            def transpose_probs(n, i):
                pe.wait_ge(normed, n + 1)
                if some(n):
                    pe.wait_ge(pT_stored, n)
                for c in range(3):
                    op = nc.tensor.transpose(pT_ps[:, P * c:P * c + P], probs[:, i % 2, P * c:P * c + P], ident[:, :])
                op.then_inc(pT_done, 1)

            def down(b, i):
                n = STEPS * b + i
                if i == 0:
                    if some(b):
                        pe.wait_ge(ffn_done, b)
                pe.wait_ge(i_split, n + 1)
                w = w_hi[:, i // 2, i % 2, DOWNW, :], w_lo[:, i // 2, i % 2, DOWNW, :]
                for tt in range(TT):
                    hidden = i_hi[:, i % 4, P * tt:P * tt + P], i_lo[:, i % 4, P * tt:P * tt + P]
                    op = product(acc[:, D * tt:D * tt + D], pieces(hidden, w), begin=i == 0 and tt == 0,
                                 end=i == STEPS - 1, loose=True)
                op.then_inc(down_done, 1)

            def attend(b, par, g):
                pe.wait_ge(pT_stored, STEPS * b + 4 * g + 4)
                if g == 0:
                    pe.wait_ge(v_stored, 4 * (b + 1))
                    if some(b):
                        pe.wait_ge(o_split, b)
                tile, odd = divmod(g, 2)
                for kt, (c0, c1, first_token) in enumerate(((0, S, 0), (S, 3 * P, P))):
                    for quadrant in range(4):
                        i = 4 * g + quadrant
                        r = 32 * quadrant
                        op = nc.tensor.matmul(o_ps[r:r + 32, S * tile + first_token:S * tile + S],
                                              v_pad[:, par, kt, head_of(i), :], pT[:, i % 8, c0:c1],
                                              start=odd == 0 and kt == 0, stop=odd == 1 and kt == 1, skip_group_check=True)
                op.then_inc(pv_done, 1)

            def project(b, batches):
                pe.wait_ge(aw_ready, 3)
                pe.wait_ge(o_split, b + 1)
                pe.wait_ge(v_stored, 4 * batches)
                for tt in range(TT):
                    tokens = slice(P * tt, P * tt + P)
                    op = product(m1[:, D * tt:D * tt + D],
                                 [p for t in range(2) for p in
                                  pieces((o_hi[:, t, tokens], o_lo[:, t, tokens]), aws(A_WO + D * t, A_WO + D * t + D))])
                op.then_inc(wo_done, 1)

            def batch(b, par, first, last):
                for i in range(STEPS):
                    n = STEPS * b + i
                    scores(b, par, i, first)
                    gate_up(b, par, i, first)
                    if i >= 2:
                        down(b, i - 2)
                    elif not first:
                        down(b - 1, STEPS - 2 + i)
                    if not (first and i == 0):
                        transpose_probs(n - 1, (i - 1) % STEPS)
                    if i == 1 and not first:
                        attend(b - 1, 1 - par, GROUPS - 1)
                    if i in (5, 9, 13):
                        attend(b, par, i // 4 - 1)
                    if i == 4 and not first:
                        project(b - 1, b + 1)
                    if not last:
                        if i == 3:
                            transpose_tokens(b + 1)
                        if i == 6:
                            latent(b + 1, 1 - par)
                        if i in (7, 8):
                            queries(b + 1, 1 - par, i - 7)
                        if i == 10:
                            keys(b + 1)
                        if i == 11:
                            values(b + 1)

            pe.wait_ge(const_ready, 5)
            transpose_tokens(0)
            pe.wait_ge(aw_ready, 1)
            latent(0, 0)
            queries(0, 0, 0)
            queries(0, 0, 1)
            pe.wait_ge(aw_ready, 2)
            keys(0)
            values(0)
            batch(0, 0, True, False)
            with pe.Fori(0, (B - 2) // 2) as it:
                batch(2 * it + 1, 1, False, False)
                batch(2 * it + 2, 0, False, False)
            batch(B - 1, 1, False, True)
            transpose_probs(STEPS * B - 1, STEPS - 1)
            down(B - 1, STEPS - 2)
            attend(B - 1, 1, GROUPS - 1)
            down(B - 1, STEPS - 1)
            project(B - 1, B)


def kernel(**inputs):
    import numpy as _np
    import concourse.bacc as _bacc
    from concourse.bass_utils import run_bass_kernel_spmd as _run

    a = {k.removeprefix("L0_"): _np.asarray(v) for k, v in inputs.items()}
    def by_byte(w):
        return w.reshape(CHUNKS, P, 2, -1).transpose(3, 0, 2, 1).reshape(-1, CHUNKS, 2 * P)

    def by_unit(w):
        return w.T.reshape(CHUNKS, -1, D).transpose(1, 0, 2)

    packed = _np.stack([by_byte(a["ffn_gate_W_packed"]), by_byte(a["ffn_up_W_packed"]), by_unit(a["ffn_down_W_packed"])], axis=2)
    scales = _np.stack([by_byte(a["ffn_gate_scales"]), by_byte(a["ffn_up_scales"]), by_unit(a["ffn_down_scales"])], axis=2)
    arrays = {
        "x": a["attn_x"], "wq": a["attn_Wq"], "wkv": a["attn_Wkv"], "wk": a["attn_Wk"], "wv": a["attn_Wv"], "wo": a["attn_Wo"],
        "packed": packed.reshape(P, CHUNKS, 3 * S), "scales": scales.reshape(P // 16, CHUNKS, 3 * S),
    }
    arrays = {k: _np.ascontiguousarray(v) for k, v in arrays.items()}
    nc = _bacc.Bacc("TRN2", target_bir_lowering=False, num_devices=1)
    aps = [nc.dram_tensor(k, v.shape, mybir.dt.from_np(v.dtype), kind="ExternalInput").ap() for k, v in arrays.items()]
    out = nc.dram_tensor("out", (B, S, D), F32, kind="ExternalOutput").ap()
    layer(nc, *aps, out)
    return _run(nc, [arrays], core_ids=[0]).results[0]["out"]
```
